# Optimizing a Trainium2 kernel written in Bass

```python
import numpy as np
import jax
import jax.numpy as jnp

def _softmax(x, axis=-1):
    return jax.nn.softmax(x, axis=axis)

def _gelu(x):
    return jax.nn.gelu(x, approximate=True)

def _silu(x):
    return jax.nn.silu(x)

def _sigmoid(x):
    return jax.nn.sigmoid(x)

def _layernorm(x, axis=-1, eps=1e-05):
    m = jnp.mean(x, axis=axis, keepdims=True)
    v = jnp.var(x, axis=axis, keepdims=True)
    return (x - m) / jnp.sqrt(v + eps)

def _scatter_add(tgt, idx, src, axis=0):
    return tgt.at[idx].add(src)

def _segment_sum(src, seg, n):
    return jax.ops.segment_sum(src, seg, n)
kernel_name = 'mk_perceiver_d1_seqx_r2_0ef1a9'

def setup_inputs(seed: int=0):
    np.random.seed(seed)
    _w = jnp.asarray

    def _rec_inputs():
        import jax
        import jax.numpy as jnp
        _rk = jax.random.key(seed)
        x = -0.0002928 + 1 * jax.random.normal(jax.random.fold_in(_rk, 1), (1, 512, 512), jnp.float32)
        _lenS = 512 - jax.random.randint(jax.random.fold_in(_rk, 7), (1,), 0, max(1, 512 // 4) + 1, jnp.int32)
        _lenS2 = 8192 - jax.random.randint(jax.random.fold_in(_rk, 8), (1,), 0, max(1, 8192 // 4) + 1, jnp.int32)
        _ctx_1024P = jax.random.normal(jax.random.fold_in(_rk, 11), (1, 16, 512), jnp.float32)
        _ctx_1024c = jax.random.dirichlet(jax.random.fold_in(_rk, 511), 0.3 * jnp.ones((16,), jnp.float32), (1, 8192))
        _ctx_1024t = jnp.einsum('bsk,bkd->bsd', _ctx_1024c, _ctx_1024P)
        _ctx_1024t = _ctx_1024t * jax.lax.rsqrt(jnp.mean(jnp.square(_ctx_1024t)) + 1e-12) * 0.953939
        ctx_1024 = -1.39393e-06 + 0.999914 * (_ctx_1024t + 0.3 * jax.random.normal(jax.random.fold_in(_rk, 611), (1, 8192, 512), jnp.float32))
        return (x, ctx_1024)
    x, ctx_1024 = _rec_inputs()

    def _L0_xattn_setup():
        import jax, jax.numpy as jnp
        import numpy as np
        D_MODEL = 512
        N_HEADS = 16
        key = jax.random.key(seed)
        ks = jax.random.split(key, 11)
        B, L, S, D = (2, 1024, 1024, D_MODEL)
        s = 1.0 / np.sqrt(D)
        return {'Q': jax.random.normal(ks[0], (B, L, D), jnp.float32), 'K': jax.random.normal(ks[1], (B, S, D), jnp.float32), 'V': jax.random.normal(ks[2], (B, S, D), jnp.float32), 'Wq': jax.random.normal(ks[3], (D, D), jnp.float32) * s, 'bq': jnp.zeros((D,), jnp.float32), 'Wk': jax.random.normal(ks[4], (D, D), jnp.float32) * s, 'bk': jnp.zeros((D,), jnp.float32), 'Wv': jax.random.normal(ks[5], (D, D), jnp.float32) * s, 'bv': jnp.zeros((D,), jnp.float32), 'We': jax.random.normal(ks[6], (D, D), jnp.float32) * s, 'be': jnp.zeros((D,), jnp.float32)}
    _L0_xattn_all = _L0_xattn_setup()
    _L0_xattn_in = {k: v for k, v in _L0_xattn_all.items() if k in ('Wq', 'bq', 'Wk', 'bk', 'Wv', 'bv', 'We', 'be')}
    del _L0_xattn_all

    def _L0_attn_setup():
        import jax, jax.numpy as jnp
        import numpy as np
        EPS = 1e-12
        key = jax.random.key(seed)
        k1, k2 = jax.random.split(key)
        b, n, d = (4, 2048, 512)
        x = jax.random.normal(k1, (b, n, d), dtype=jnp.float32)
        W_qkva = jax.random.normal(k2, (3 * d, d), dtype=jnp.float32) * 0.02
        gamma = jnp.ones((d,), dtype=jnp.float32)
        return {'x': x, 'W_qkva': W_qkva, 'gamma': gamma}
    _L0_attn_all = _L0_attn_setup()
    _L0_attn_in = {k: v for k, v in _L0_attn_all.items() if k in ('W_qkva', 'gamma')}
    del _L0_attn_all

    def _L0_ffn_setup():
        import jax, jax.numpy as jnp
        import numpy as np
        TOP_K = 4
        key = jax.random.key(seed)
        ks = jax.random.split(key, 6)
        B, S, H, I, E = (2, 512, 512, 512, 16)
        SD = I * 1
        s = 0.02
        return {'hidden_states': jax.random.normal(ks[0], (B, S, H), jnp.float32), 'gate_w': jax.random.normal(ks[1], (E, H), jnp.float32) * s, 'w1': jax.random.normal(ks[2], (E, I, H), jnp.float32) * s, 'w2': jax.random.normal(ks[3], (E, H, I), jnp.float32) * s, 'shared_gu': jax.random.normal(ks[4], (2 * SD, H), jnp.float32) * s, 'shared_down': jax.random.normal(ks[5], (H, SD), jnp.float32) * s}
    _L0_ffn_all = _L0_ffn_setup()
    _L0_ffn_in = {k: v for k, v in _L0_ffn_all.items() if k in ('gate_w', 'w1', 'w2', 'shared_gu', 'shared_down')}
    del _L0_ffn_all
    return {'x': x, 'ctx_1024': ctx_1024, 'L0_xattn_Wq': _L0_xattn_in['Wq'], 'L0_xattn_bq': _L0_xattn_in['bq'], 'L0_xattn_Wk': _L0_xattn_in['Wk'], 'L0_xattn_bk': _L0_xattn_in['bk'], 'L0_xattn_Wv': _L0_xattn_in['Wv'], 'L0_xattn_bv': _L0_xattn_in['bv'], 'L0_xattn_We': _L0_xattn_in['We'], 'L0_xattn_be': _L0_xattn_in['be'], 'L0_attn_W_qkva': _L0_attn_in['W_qkva'], 'L0_attn_gamma': _L0_attn_in['gamma'], 'L0_ffn_gate_w': _L0_ffn_in['gate_w'], 'L0_ffn_w1': _L0_ffn_in['w1'], 'L0_ffn_w2': _L0_ffn_in['w2'], 'L0_ffn_shared_gu': _L0_ffn_in['shared_gu'], 'L0_ffn_shared_down': _L0_ffn_in['shared_down']}

def reference(x, ctx_1024, L0_xattn_Wq, L0_xattn_bq, L0_xattn_Wk, L0_xattn_bk, L0_xattn_Wv, L0_xattn_bv, L0_xattn_We, L0_xattn_be, L0_attn_W_qkva, L0_attn_gamma, L0_ffn_gate_w, L0_ffn_w1, L0_ffn_w2, L0_ffn_shared_gu, L0_ffn_shared_down):
    import jax
    import jax.numpy as jnp

    def _L0_xattn_ref(Q, K, V, Wq, bq, Wk, bk, Wv, bv, We, be):
        import jax, jax.numpy as jnp
        import numpy as np
        D_MODEL = 512
        N_HEADS = 16
        B, L, D = Q.shape
        S = K.shape[1]
        H = N_HEADS
        E = D // H
        q = (Q @ Wq + bq).reshape(B, L, H, E)
        k = (K @ Wk + bk).reshape(B, S, H, E)
        v = (V @ Wv + bv).reshape(B, S, H, E)
        scale = 1.0 / np.sqrt(E)
        scores = jnp.einsum('blhe,bshe->bhls', q, k)
        A = jax.nn.softmax(scale * scores, axis=-1)
        out = jnp.einsum('bhls,bshd->blhd', A, v).reshape(B, L, H * E)
        return out @ We + be

    def _L0_attn_ref(x, W_qkva, gamma):
        import jax, jax.numpy as jnp
        import numpy as np
        EPS = 1e-12
        d = gamma.shape[0]
        scale = d ** 0.5
        norm = jnp.maximum(jnp.linalg.norm(x, axis=-1, keepdims=True), EPS)
        xn = x / norm * scale * gamma
        h = jnp.einsum('bnd,ed->bne', xn, W_qkva)
        q, kv, a = jnp.split(h, 3, axis=-1)
        a = jax.nn.sigmoid(a)

        def binop(e_i, e_j):
            a_i, kv_i = e_i
            a_j, kv_j = e_j
            return (a_j * a_i, a_j * kv_i + kv_j)
        _, y = jax.lax.associative_scan(binop, (a, kv), axis=1)
        return q * y

    def _L0_ffn_ref(hidden_states, gate_w, w1, w2, shared_gu, shared_down):
        import jax, jax.numpy as jnp
        import numpy as np
        TOP_K = 4
        orig_shape = hidden_states.shape
        H = orig_shape[-1]
        x = hidden_states.reshape(-1, H)
        T = x.shape[0]
        E = gate_w.shape[0]
        logits = x @ gate_w.T
        probs = jax.nn.softmax(logits, axis=-1)
        topv, topi = jax.lax.top_k(probs, TOP_K)
        topv = topv / jnp.sum(topv, axis=-1, keepdims=True)
        W = jnp.zeros((T, E), x.dtype).at[jnp.arange(T)[:, None], topi].set(topv)
        h = jax.nn.silu(jnp.einsum('th,eih->tei', x, w1))
        routed = jnp.einsum('tei,ehi,te->th', h, w2, W)
        gu = x @ shared_gu.T
        gate, up = jnp.split(gu, 2, axis=-1)
        shared = jax.nn.silu(gate) * up @ shared_down.T
        return (routed + shared).reshape(orig_shape)
    x = x + _L0_xattn_ref(_layernorm(x, axis=-1), ctx_1024, ctx_1024, L0_xattn_Wq, L0_xattn_bq, L0_xattn_Wk, L0_xattn_bk, L0_xattn_Wv, L0_xattn_bv, L0_xattn_We, L0_xattn_be)
    x = x + _L0_attn_ref(_layernorm(x, axis=-1), L0_attn_W_qkva, L0_attn_gamma)
    x = x + _L0_ffn_ref(_layernorm(x, axis=-1), L0_ffn_gate_w, L0_ffn_w1, L0_ffn_w2, L0_ffn_shared_gu, L0_ffn_shared_down)
    return x

_drawn_inputs = setup_inputs


def setup_inputs(seed=0):
    import zlib

    import numpy as np

    out = dict(_drawn_inputs(seed))
    spreads = {'L0_xattn_bq': (0.0, 0.362),
     'L0_xattn_bk': (0.0, 0.8),
     'L0_xattn_bv': (0.0, 0.1),
     'L0_xattn_be': (0.0, 0.1),
     'L0_attn_gamma': (1.0, 0.2)}
    factors = {}
    for name, (base, spread) in spreads.items():
        noise = np.random.default_rng([zlib.crc32(name.encode()), seed]).standard_normal(out[name].shape)
        drawn = base * np.exp(spread * noise) if base else spread * noise
        out[name] = jnp.asarray(drawn.astype(out[name].dtype))
    for name, factor in factors.items():
        out[name] = (out[name] * factor).astype(out[name].dtype)
    return out
```

```python
from contextlib import ExitStack

import concourse.bass as bass
from concourse import mybir

F32 = mybir.dt.float32
F32R = mybir.dt.float32r
ALU = mybir.AluOpType
ACT = mybir.ActivationFunctionType
AX = mybir.AxisListType

P = 128
D = 512
KT = D // P
T = 512
TT = T // P
S = 8192
H = 16
E = D // H
CH = 512
NCH = S // CH
KEYT = S // P
NG = KEYT // 4
QUARTERS = 4
QK = S // QUARTERS
NEXP = 16
TOPK = 4
LN_EPS = 1e-5
NORM_EPS = 1e-12
SCALE = float(E) ** -0.5

PASS1_GROUPS = 14


def pass1_items(g):
    n = NCH * TT
    lo = min(n, g * n // PASS1_GROUPS)
    hi = min(n, (g + 1) * n // PASS1_GROUPS)
    return [(k // TT, k % TT) for k in range(lo, hi)]


def wait(eng, sem, value):
    if isinstance(value, int) and value <= 0:
        return
    eng.wait_ge(sem, value)


def perceiver_program(nc, x, ctxT, wq, bq, wk, bk, wv, bv, we, be, w_qkvaT, gamma, gate_wT, w1T, w2T,
                      sguT, sdownT, out):
    def rows(ap):
        return ap.rearrange("(k p) n -> p k n", p=P)

    kh_d = nc.dram_tensor("kh_scratch", (D, S), F32, kind="Internal").ap()
    kl_d = nc.dram_tensor("kl_scratch", (D, S), F32, kind="Internal").ap()
    qh_d = nc.dram_tensor("qh_scratch", (D, T), F32, kind="Internal").ap()
    ql_d = nc.dram_tensor("ql_scratch", (D, T), F32, kind="Internal").ap()
    v_d = nc.dram_tensor("v_scratch", (H, P, KEYT * E), F32, kind="Internal").ap()
    att_d = nc.dram_tensor("att_scratch", (D, T), F32, kind="Internal").ap()

    with ExitStack() as whole:
        def alloc(ctx):
            return (lambda name, shape, dt=F32: ctx.enter_context(nc.sbuf_tensor(name, shape, dt)))

        def sem(name):
            return whole.enter_context(nc.semaphore(name))

        sb = alloc(whole)
        psum = whole.enter_context(nc.psum_tensor("psum", [P, 8, 512], F32))

        X = sb("X", [P, TT, D])
        XN = sb("XN", [P, TT, D])
        AH = sb("AH", [P, KT, T], F32R)
        AL = sb("AL", [P, KT, T], F32R)
        ident = sb("ident", [P, P])
        stats = sb("stats", [P, TT, 6])
        mv = sb("mv", [P, TT, 2])
        ve = sb("ve", [P, TT])
        sd = sb("sd", [P, TT])
        rs = sb("rs", [P, TT])
        t0 = sb("t0", [P, TT])
        bcol = sb("bcol", [P, 3, KT])
        brow = sb("brow", [P, 2, D])

        s_ident = sem("s_ident")
        s_x = sem("s_x")
        s_small = sem("s_small")
        dve_step = sem("dve_step")
        dve_ve = sem("dve_ve")
        act_sqrt = sem("act_sqrt")
        pe_tr = sem("pe_tr")
        act_hi = sem("act_hi")
        dve_lo = sem("dve_lo")
        dve_xn = sem("dve_xn")

        steps = [0]

        def link(eng, ins):
            steps[0] += 1
            ins.then_inc(dve_step, 1)
            eng.wait_ge(dve_step, steps[0])

        roots = [0]

        def inverse_root_dve(eng):
            roots[0] += 1
            eng.wait_ge(act_sqrt, roots[0])
            link(eng, eng.reciprocal(t0[:, :], sd[:, :]))
            link(eng, eng.tensor_tensor(t0[:, :], t0[:, :], ve[:, :], ALU.mult))
            link(eng, eng.tensor_tensor(t0[:, :], t0[:, :], sd[:, :], ALU.add))
            link(eng, eng.tensor_scalar(t0[:, :], t0[:, :], 0.5, None, ALU.mult))
            link(eng, eng.reciprocal(rs[:, :], t0[:, :]))

        def layer_norm_dve(eng):
            for t in range(TT):
                ins = eng.bn_stats(stats[:, t, :], X[:, t, :])
            link(eng, ins)
            for t in range(TT):
                ins = eng.bn_aggr(mv[:, t, :], stats[:, t, :])
            link(eng, ins)
            eng.tensor_scalar(ve[:, :], mv[:, :, 1], LN_EPS, None, ALU.add).then_inc(dve_ve, 1)
            inverse_root_dve(eng)
            for t in range(TT):
                eng.tensor_scalar(XN[:, t, :], X[:, t, :], mv[:, t, 0:1], rs[:, t:t + 1],
                                  ALU.subtract, ALU.mult).then_inc(dve_xn, 1)

        def root_act(eng, n):
            eng.wait_ge(dve_ve, n)
            eng.activation(sd[:, :], ve[:, :], ACT.Sqrt).then_inc(act_sqrt, 1)

        def transpose_pe(eng, first_bank=0):
            for k in range(KT):
                for t in range(TT):
                    ins = eng.transpose(psum[:, first_bank + k, t * P:(t + 1) * P], XN[:, t, k * P:(k + 1) * P],
                                        ident[:, :])
                ins.then_inc(pe_tr, 1)

        def product3(eng, bank_ap, lh, ll, rh, rl, m=None):
            n = 0
            for k in range(KT):
                for left, right in ((lh, rh), (lh, rl), (ll, rh)):
                    ins = eng.matmul(bank_ap, left[:, k, m], right[:, k, :], start=(n == 0), stop=(n == 3 * KT - 1))
                    n += 1
            return ins

        with ExitStack() as ctx:
            sb1 = alloc(ctx)
            wraw = sb1("wraw", [P, 3, KT, D])
            wh = sb1("wh", [P, 3, KT, D], F32R)
            wl = sb1("wl", [P, 3, KT, D], F32R)
            craw = sb1("craw", [P, 2, KT, CH])
            chi = sb1("chi", [P, 2, KT, CH], F32R)
            clo = sb1("clo", [P, 2, KT, CH], F32R)
            q32 = craw[:, 0, :, :]
            khi = sb1("khi", [P, KT, CH], F32R)
            klo = sb1("klo", [P, KT, CH], F32R)
            vsb = sb1("vsb", [P, H, 4, E])

            s_w = [sem(f"s_w{n}") for n in range(3)]
            act_wh = sem("act_wh")
            pool_wl = sem("pool_wl")
            pe_q = sem("pe_q")
            dve_q = sem("dve_q")
            dve_ql = sem("dve_ql")
            act_qh = sem("act_qh")
            s_qst = sem("s_qst")
            s_c = [sem(f"s_c{n}") for n in range(2)]
            act_ch = sem("act_ch")
            dve_cl = sem("dve_cl")
            pe_k = sem("pe_k")
            pe_v = sem("pe_v")
            act_kh = sem("act_kh")
            dve_kl = sem("dve_kl")
            dve_v = sem("dve_v")
            s_kst = sem("s_kst")
            s_vst = sem("s_vst")

            block = ctx.enter_context(nc.Block())

            @block.sync
            def _(eng):
                eng.dma_start(X[:, :, :], x.rearrange("(k p) n -> p k n", p=P)).then_inc(s_x, 16)
                for n, w in enumerate((wq, wk, wv)):
                    eng.dma_start(wraw[:, n, :, :], rows(w)).then_inc(s_w[n], 16)
                eng.dma_start(bcol[:, 0, :], bq).then_inc(s_small, 16)
                eng.dma_start(bcol[:, 1, :], bk).then_inc(s_small, 16)
                eng.dma_start(bcol[:, 2, :], gamma).then_inc(s_small, 16)
                eng.dma_start(brow[:, 0, :], bv.to_broadcast([P, D])).then_inc(s_small, 16)
                eng.dma_start(brow[:, 1, :], be.to_broadcast([P, D])).then_inc(s_small, 16)

                eng.dma_start(craw[:, 1, :, :], rows(ctxT)[:, :, CH:2 * CH]).then_inc(s_c[1], 16)
                eng.wait_ge(act_qh, KT)
                eng.wait_ge(dve_ql, KT)
                eng.dma_start(craw[:, 0, :, :], rows(ctxT)[:, :, 0:CH]).then_inc(s_c[0], 16)
                with eng.Fori(1, NCH // 2) as i:
                    for u in range(2):
                        eng.wait_ge(dve_cl, i * 2 + u - 1)
                        eng.dma_start(craw[:, u, :, :], rows(ctxT)[:, :, bass.ds((i * 2 + u) * CH, CH)])\
                           .then_inc(s_c[u], 16)

            @block.gpsimd
            def _(eng):
                eng.memset(ident[:, :], 0.0).then_inc(s_ident, 1)
                eng.wait_ge(s_ident, 1)
                eng.affine_select(out=ident[:, :], in_=ident[:, :], compare_op=ALU.not_equal, fill=1.0, base=0,
                                  pattern=[[-1, P]], channel_multiplier=1).then_inc(s_ident, 1)
                for n in range(3):
                    eng.wait_ge(act_wh, n + 1)
                    eng.tensor_tensor(wl[:, n, :, :], wraw[:, n, :, :], wh[:, n, :, :].bitcast(F32), ALU.subtract)\
                       .then_inc(pool_wl, 1)

            @block.scalar
            def _(eng):
                for n in range(3):
                    eng.wait_ge(s_w[n], 16)
                    eng.activation(wh[:, n, :, :], wraw[:, n, :, :], ACT.Copy).then_inc(act_wh, 1)
                root_act(eng, 1)
                for k in range(KT):
                    eng.wait_ge(pe_tr, k + 1)
                    eng.activation(AH[:, k, :], psum[:, k, :], ACT.Copy).then_inc(act_hi, 1)
                for m in range(KT):
                    eng.wait_ge(dve_q, m + 1)
                    eng.activation(chi[:, 0, m, :], q32[:, m, :], ACT.Copy).then_inc(act_qh, 1)
                eng.wait_ge(act_qh, KT)
                eng.dma_start(rows(qh_d), chi[:, 0, :, :].bitcast(F32)).then_inc(s_qst, 16)
                eng.wait_ge(dve_ql, KT)
                eng.dma_start(rows(ql_d), clo[:, 0, :, :].bitcast(F32)).then_inc(s_qst, 16)
                eng.wait_ge(s_qst, 32)

                def split(i, u):
                    c = i * 2 + u
                    eng.wait_ge(s_c[u], 16 * i + 16)
                    wait(eng, pe_v, 4 * (c - 1))
                    eng.activation(chi[:, u, :, :], craw[:, u, :, :], ACT.Copy).then_inc(act_ch, 1)

                def chunk(i, u, last=False):
                    c = i * 2 + u
                    if not last:
                        split(i + u, 1 - u)
                    wait(eng, s_kst, 32 * c)
                    for m in range(KT):
                        eng.wait_ge(pe_k, 4 * c + m + 1)
                        eng.activation(khi[:, m, :], psum[:, m, :], ACT.Identity, bias=bcol[:, 1, m:m + 1])\
                           .then_inc(act_kh, 1)
                    cols = bass.ds(c * CH, CH)
                    eng.wait_ge(act_kh, 4 * c + 4)
                    eng.dma_start(rows(kh_d)[:, :, cols], khi[:, :, :].bitcast(F32)).then_inc(s_kst, 16)
                    eng.wait_ge(dve_kl, 4 * c + 4)
                    eng.dma_start(rows(kl_d)[:, :, cols], klo[:, :, :].bitcast(F32)).then_inc(s_kst, 16)
                    eng.wait_ge(dve_v, 4 * c + 4)
                    eng.dma_start(v_d.rearrange("h p n -> p h n")[:, :, bass.ds(c * 4 * E, 4 * E)],
                                  vsb[:, :, :, :].rearrange("p h t e -> p h (t e)")).then_inc(s_vst, 16)

                split(0, 0)
                chunk(0, 0)
                chunk(0, 1)
                with eng.Fori(1, NCH // 2 - 1) as i:
                    chunk(i, 0)
                    chunk(i, 1)
                chunk(NCH // 2 - 1, 0)
                chunk(NCH // 2 - 1, 1, last=True)
                eng.wait_ge(s_kst, 32 * NCH)
                eng.wait_ge(s_vst, 16 * NCH)

            @block.tensor
            def _(eng):
                eng.wait_ge(s_ident, 2)
                eng.wait_ge(dve_xn, TT)
                transpose_pe(eng)
                eng.wait_ge(act_hi, KT)
                eng.wait_ge(dve_lo, KT)
                eng.wait_ge(act_wh, 1)
                eng.wait_ge(pool_wl, 1)
                for m in range(KT):
                    product3(eng, psum[:, 4 + m, :], wh[:, 0, :, :], wl[:, 0, :, :], AH, AL,
                             slice(m * P, (m + 1) * P)).then_inc(pe_q, 1)
                eng.wait_ge(act_wh, 3)
                eng.wait_ge(pool_wl, 3)

                def chunk(i, u):
                    c = i * 2 + u
                    eng.wait_ge(act_ch, c + 1)
                    eng.wait_ge(dve_cl, c + 1)
                    ch, cl = chi[:, u, :, :], clo[:, u, :, :]
                    for m in range(KT):
                        wait(eng, dve_kl, 4 * (c - 1) + m + 1)
                        product3(eng, psum[:, m, :], wh[:, 1, :, :], wl[:, 1, :, :], ch, cl,
                                 slice(m * P, (m + 1) * P)).then_inc(pe_k, 1)
                    for t in range(4):
                        if isinstance(c, int) and c == 0:
                            eng.wait_ge(dve_q, KT)
                        wait(eng, dve_v, 4 * (c - 1) + t + 1)
                        product3(eng, psum[:, 4 + t, :], ch, cl, wh[:, 2, :, :], wl[:, 2, :, :],
                                 slice(t * P, (t + 1) * P)).then_inc(pe_v, 1)

                chunk(0, 0)
                chunk(0, 1)
                with eng.Fori(1, NCH // 2) as i:
                    chunk(i, 0)
                    chunk(i, 1)

            @block.vector
            def _(eng):
                eng.wait_ge(s_x, 16)
                layer_norm_dve(eng)
                for k in range(KT):
                    eng.wait_ge(act_hi, k + 1)
                    eng.tensor_tensor(AL[:, k, :], psum[:, k, :], AH[:, k, :].bitcast(F32), ALU.subtract)\
                       .then_inc(dve_lo, 1)
                eng.wait_ge(s_small, 16 * 5)
                for m in range(KT):
                    eng.wait_ge(pe_q, m + 1)
                    eng.tensor_scalar(q32[:, m, :], psum[:, 4 + m, :], bcol[:, 0, m:m + 1], SCALE,
                                      ALU.add, ALU.mult).then_inc(dve_q, 1)
                for m in range(KT):
                    eng.wait_ge(act_qh, m + 1)
                    eng.tensor_tensor(clo[:, 0, m, :], q32[:, m, :], chi[:, 0, m, :].bitcast(F32), ALU.subtract)\
                       .then_inc(dve_ql, 1)
                eng.wait_ge(s_qst, 32)

                def split(c, u):
                    eng.wait_ge(act_ch, c + 1)
                    eng.tensor_tensor(clo[:, u, :, :], craw[:, u, :, :], chi[:, u, :, :].bitcast(F32), ALU.subtract)\
                       .then_inc(dve_cl, 1)

                def chunk(i, u, last=False):
                    c = i * 2 + u
                    if not last:
                        split(c + 1, 1 - u)
                    for m in range(KT):
                        eng.wait_ge(act_kh, 4 * c + m + 1)
                        eng.scalar_tensor_tensor(out=klo[:, m, :], in0=psum[:, m, :], scalar=bcol[:, 1, m:m + 1],
                                                 in1=khi[:, m, :].bitcast(F32), op0=ALU.add, op1=ALU.subtract)\
                           .then_inc(dve_kl, 1)
                    wait(eng, s_vst, 16 * c)
                    for t in range(4):
                        eng.wait_ge(pe_v, 4 * c + t + 1)
                        eng.tensor_tensor(vsb[:, :, t, :], psum[:, 4 + t, :].rearrange("p (h e) -> p h e", e=E),
                                          brow[:, 0, :].rearrange("p (h e) -> p h e", e=E), ALU.add)\
                           .then_inc(dve_v, 1)

                split(0, 0)
                chunk(0, 0)
                chunk(0, 1)
                with eng.Fori(1, NCH // 2 - 1) as i:
                    chunk(i, 0)
                    chunk(i, 1)
                chunk(NCH // 2 - 1, 0)
                chunk(NCH // 2 - 1, 1, last=True)

        with ExitStack() as ctx:
            sb2 = alloc(ctx)
            ks = [sb2(f"ks{n}", [P, S], F32R) for n in range(2)]
            qmax = [sb2(f"qmax{n}", [P, T], F32R) for n in range(2)]
            qexp = [sb2(f"qexp{n}", [P, T], F32R) for n in range(2)]
            vh = [sb2(f"vh{n}", [P, KEYT, E]) for n in range(2)]
            prob = sb2("prob", [P, 4, 2, T])
            pool_sum = sb2("pool_sum", [P, 2, T])
            dve_sum = sb2("dve_sum", [P, T])
            ones = sb2("ones", [P, E])
            sel = sb2("sel", [P, E])
            mx = sb2("mx", [P, TT, NCH])
            m4 = sb2("m4", [P, TT])
            nm = sb2("nm", [P, TT, E], F32R)
            osb = sb2("osb", [P, T])
            dsb = sb2("dsb", [P, T])
            rden = sb2("rden", [E, T])
            att = [sb2(f"att{n}", [E, T]) for n in range(2)]

            const_c = sem("const_c")
            s_kq = [[sem(f"s_k{n}q{q}") for q in range(QUARTERS)] for n in range(2)]
            s_q1 = [sem(f"s_q1_{n}") for n in range(2)]
            s_q2 = [sem(f"s_q2_{n}") for n in range(2)]
            s_vh = [sem(f"s_vh{n}") for n in range(2)]
            st_ready = sem("st_ready")
            exp_done = sem("exp_done")
            pv_done = sem("pv_done")
            ring_ready = sem("ring_ready")
            ring_free = sem("ring_free")
            pool_added = sem("pool_added")
            dve_added = sem("dve_added")
            nm_zero = sem("nm_zero")
            nm_ready = sem("nm_ready")
            max_step = sem("max_step")
            od_out = sem("od_out")
            s_attst = [sem(f"s_attst{n}") for n in range(2)]

            ITEMS = NCH * TT + 1 + 2

            def ring_base(h):
                if isinstance(h, int) and h == 0:
                    return NCH * TT + 1
                return h * ITEMS + NCH * TT - 1

            def ring_items(h, first, last):
                out = []
                for g in range(NG):
                    if not last:
                        out += [(g, "max", kc, qt) for kc, qt in pass1_items(g)]
                    if g == 1 and not first:
                        out += [(g, "den", 0, 0), (g, "sum", 0, 0)]
                    if g == NG - 1 and not last:
                        out += [(g, "neg", 0, 0)]
                return out

            ring_end = ring_base(H - 1) + 2

            RING = (6, 7)
            OUT, DEN = 4, 5

            block = ctx.enter_context(nc.Block())

            def head_rows(ap, h):
                return ap[bass.ds(h * E, E), :]

            @block.sync
            def _(eng):
                def load_quarter(h, n, q):
                    cols = slice(q * QK, (q + 1) * QK)
                    for part, src in enumerate((kh_d, kh_d, kl_d)):
                        eng.dma_start(ks[n][part * E:(part + 1) * E, cols].bitcast(F32), head_rows(src, h)[:, cols])\
                           .then_inc(s_kq[n][q], 16)

                def load_q(h, tile, s):
                    for part, src in enumerate((qh_d, ql_d, qh_d)):
                        eng.dma_start(tile[part * E:(part + 1) * E, :].bitcast(F32), head_rows(src, h))\
                           .then_inc(s, 16)

                def load_v(h, n):
                    eng.dma_start(vh[n][:, :, :].rearrange("p t e -> p (t e)"), v_d[h, :, :]).then_inc(s_vh[n], 16)

                load_q(0, qmax[0], s_q1[0])
                for q in range(QUARTERS):
                    load_quarter(0, 0, q)
                load_q(0, qexp[0], s_q2[0])
                load_v(0, 0)
                load_q(1, qmax[1], s_q1[1])
                for q in range(QUARTERS):
                    load_quarter(1, 1, q)

                def store(h, u, count):
                    eng.wait_ge(ring_free, count)
                    eng.dma_start(head_rows(att_d, h), att[u][:, :]).then_inc(s_attst[u], 16)

                def sum_taken(last):
                    return [n for n, it in enumerate(ring_items(1, False, last)) if it[1] == "sum"][0] + 1

                def step(i, u, first=False, has_next=True, has_next2=True):
                    h = i * 2 + u
                    if has_next2:
                        eng.wait_ge(nm_ready, h + 1)
                        load_q(h + 2, qmax[u], s_q1[u])
                    if has_next:
                        wait(eng, pv_done, NG * h)
                        load_q(h + 1, qexp[1 - u], s_q2[1 - u])
                        load_v(h + 1, 1 - u)
                    if has_next2:
                        for q in range(QUARTERS):
                            eng.wait_ge(st_ready, 2 * NG * h + 2 * NG // QUARTERS * (q + 1))
                            load_quarter(h + 2, u, q)
                            if q == 0 and not first:
                                store(h - 1, 1 - u, ring_base(h) + sum_taken(False))
                    else:
                        store(h - 1, 1 - u, ring_base(h) + sum_taken(not has_next))

                step(0, 0, first=True)
                step(0, 1)
                with eng.Fori(1, H // 2 - 1) as i:
                    step(i, 0)
                    step(i, 1)
                step(H // 2 - 1, 0, has_next2=False)
                step(H // 2 - 1, 1, has_next=False, has_next2=False)
                store(H - 1, 1, ring_end + 2)
                for n in range(2):
                    eng.wait_ge(s_attst[n], 16 + 16 * H // 2)

            @block.gpsimd
            def _(eng):
                for n in range(2):
                    eng.memset(ks[n][3 * E:P, :].bitcast(F32), 0.0).then_inc(const_c, 1)
                    eng.wait_ge(const_c, 2 * n + 1)
                    eng.memset(ks[n][3 * E:3 * E + 2, :].bitcast(F32), 1.0).then_inc(const_c, 1)
                    eng.wait_ge(const_c, 2 * n + 2)
                eng.memset(ones[:, :], 1.0).then_inc(const_c, 1)
                eng.wait_ge(const_c, 5)
                eng.memset(sel[:, :], 0.0).then_inc(const_c, 1)
                for j in range(4):
                    eng.wait_ge(const_c, 6 + j)
                    eng.affine_select(out=sel[:, :], in_=sel[:, :], compare_op=ALU.not_equal, fill=1.0,
                                      base=-E * j, pattern=[[-1, E]], channel_multiplier=1).then_inc(const_c, 1)

                def step(i, u):
                    h = i * 2 + u
                    wait(eng, pv_done, NG * h)
                    for g in range(NG - 1):
                        eng.wait_ge(exp_done, h * 2 * NG + 2 * g + 2)
                        pair = prob[:, (2 * g + 1) % 4, :, :]
                        if g == 1:
                            eng.tensor_tensor(pool_sum[:, :, :], prob[:, 1, :, :], pair, ALU.add)\
                               .then_inc(pool_added, 2)
                        elif g > 1:
                            eng.wait_ge(pool_added, h * (NG - 1) + g)
                            eng.tensor_tensor(pool_sum[:, :, :], pool_sum[:, :, :], pair, ALU.add)\
                               .then_inc(pool_added, 1)

                step(0, 0)
                step(0, 1)
                with eng.Fori(1, H // 2) as i:
                    step(i, 0)
                    step(i, 1)

            @block.scalar
            def _(eng):
                def step(i, u):
                    h = i * 2 + u
                    for g in range(NG):
                        for b in range(2):
                            n = h * 2 * NG + 2 * g + b
                            eng.wait_ge(st_ready, n + 1)
                            wait(eng, pv_done, h * NG + g - 1)
                            if g != 1:
                                wait(eng, pool_added if b else dve_added, h * (NG - 1) + max(g - 1, 0))
                            eng.activation(prob[:, (2 * g + b) % 4, :, :], psum[:, 2 * b:2 * b + 2, :], ACT.Exp)\
                               .then_inc(exp_done, 1)

                step(0, 0)
                step(0, 1)
                with eng.Fori(1, H // 2) as i:
                    step(i, 0)
                    step(i, 1)

            @block.tensor
            def _(eng):
                def put(item, r, n, tile):
                    _, kind, kc, qt = item
                    out = psum[:, RING[tile], :]
                    wait(eng, ring_free, r - 1)
                    if kind == "max":
                        eng.matmul(out, qmax[n][0:3 * E, qt * P:(qt + 1) * P], ks[n][0:3 * E, kc * CH:(kc + 1) * CH],
                                   start=True, stop=True).then_inc(ring_ready, 1)
                    elif kind == "neg":
                        for t in range(TT):
                            ins = eng.matmul(psum[3 * E:P, RING[tile], t * P:(t + 1) * P], nm[:, t, :].bitcast(F32),
                                             ident[:, :], start=True, stop=True, tile_position=(0, 3 * E))
                        ins.then_inc(ring_ready, 1)
                    else:
                        src = dsb if kind == "den" else osb
                        eng.matmul(out[0:E, :], sel[:, :], src[:, :], start=True, stop=True).then_inc(ring_ready, 1)

                def maximum_item(item, r, n, tile, use):
                    _, kind, kc, qt = item
                    if kind == "max" and qt == 0 and kc % (NCH // QUARTERS) == 0:
                        if kc == 0:
                            eng.wait_ge(s_q1[n], 48 * use + 48)
                        eng.wait_ge(s_kq[n][kc // (NCH // QUARTERS)], 48 * use + 48)
                    put(item, r, n, tile)

                def column(h, bank, j, left, right, start, stop):
                    return eng.matmul(psum[j * E:(j + 1) * E, bank, :], left, right, start=start, stop=stop,
                                      tile_position=(0, j * E))

                def summed(h, u, g, b):
                    eng.wait_ge(exp_done, h * 2 * NG + 2 * g + b + 1)
                    final = g == NG - 1
                    for t in range(2):
                        ins = column(h, OUT, 2 * b + t, vh[u][:, 4 * g + 2 * b + t, :], prob[:, (2 * g + b) % 4, t, :],
                                     g == 0, final)
                    if b == 0:
                        ins = column(h, DEN, 2, ones[:, :], prob[:, (2 * g) % 4, 0, :], g == 0, False)
                    if final and b == 0:
                        ins = column(h, DEN, 3, ones[:, :], prob[:, (2 * g) % 4, 1, :], True, False)
                    if final and b == 1:
                        for t in range(2):
                            ins = column(h, DEN, t, ones[:, :], prob[:, (2 * g + 1) % 4, t, :], True, t == 1)
                        eng.wait_ge(dve_added, (h + 1) * (NG - 1))
                        eng.wait_ge(pool_added, (h + 1) * (NG - 1))
                        column(h, DEN, 2, ones[:, :], dve_sum[:, :], False, True)
                        ins = column(h, DEN, 3, ones[:, :], pool_sum[:, 0, :], False, True)
                        ins = column(h, DEN, 0, ones[:, :], pool_sum[:, 1, :], False, True)
                    if b == 1:
                        ins.then_inc(pv_done, 1)

                def step(i, u, first=False, last=False):
                    h = i * 2 + u
                    base = ring_base(h)
                    items = ring_items(h, first, last)
                    done = [0]

                    def next_items(g, count=None):
                        while done[0] < len(items) and items[done[0]][0] == g and count != 0:
                            it = items[done[0]]
                            at, tile = base + done[0], (base_parity(h, u) + done[0]) % 2
                            if it[1] == "den":
                                wait(eng, od_out, 2 * h)
                            if it[1] == "neg":
                                eng.wait_ge(nm_ready, h + 2)
                            maximum_item(it, at, 1 - u, tile, i + u)
                            done[0] += 1
                            if count is not None:
                                count -= 1

                    eng.wait_ge(s_q2[u], 48 * i + 48)
                    eng.wait_ge(ring_free, ring_base(h))
                    eng.wait_ge(s_vh[u], 16 * i + 16)
                    for g in range(NG):
                        for b in range(2):
                            n = h * 2 * NG + 2 * g + b
                            wait(eng, exp_done, n - 1)
                            for t in range(2):
                                key = (4 * g + 2 * b + t) * P
                                ins = eng.matmul(psum[:, 2 * b + t, :], ks[u][:, key:key + P], qexp[u][:, :],
                                                 start=True, stop=True)
                            ins.then_inc(st_ready, 1)
                            next_items(g, 1)
                            if g > 0:
                                if g == 1 and b == 0:
                                    wait(eng, od_out, 2 * h)
                                summed(h, u, g - 1, b)
                            elif not first:
                                summed(h - 1, 1 - u, NG - 1, b)
                            next_items(g, 1 + b if b == 0 else None)

                def base_parity(h, u):
                    return ring_base(2 + u) % 2

                eng.wait_ge(const_c, 10)
                for n, (kc, qt) in enumerate([(k // TT, k % TT) for k in range(NCH * TT)]):
                    maximum_item((0, "max", kc, qt), n, 0, n % 2, 0)
                eng.wait_ge(nm_ready, 1)
                put((0, "neg", 0, 0), NCH * TT, 0, 0)
                step(0, 0, first=True)
                step(0, 1)
                with eng.Fori(1, H // 2 - 1) as i:
                    step(i, 0)
                    step(i, 1)
                step(H // 2 - 1, 0)
                step(H // 2 - 1, 1, last=True)
                summed(H - 1, 1, NG - 1, 0)
                summed(H - 1, 1, NG - 1, 1)
                eng.wait_ge(od_out, 2 * H)
                end = ring_end
                put((0, "den", 0, 0), end, 0, end % 2)
                put((0, "sum", 0, 0), end + 1, 0, (end + 1) % 2)

            @block.vector
            def _(eng):
                eng.memset(nm[:, :, :].bitcast(F32), 0.0).then_inc(nm_zero, 1)
                for n in range(2):
                    eng.memset(att[n][:, :], 0.0).then_inc(s_attst[n], 16)

                def take(item, r, tile, h, u, i):
                    _, kind, kc, qt = item
                    src = psum[:, RING[tile], :]
                    eng.wait_ge(ring_ready, r + 1)
                    if kind == "max":
                        eng.tensor_reduce(mx[:, qt, kc:kc + 1], src, AX.X, ALU.max).then_inc(ring_free, 1)
                    elif kind == "neg":
                        eng.tensor_copy(qexp[u][3 * E:P, :], psum[3 * E:P, RING[tile], :]).then_inc(ring_free, 1)
                    elif kind == "den":
                        eng.reciprocal(rden[:, :], src[0:E, :]).then_inc(ring_free, 1)
                    else:
                        eng.wait_ge(ring_free, r)
                        eng.wait_ge(s_attst[u], 16 * i + 16)
                        eng.tensor_tensor(att[u][:, :], src[0:E, :], rden[:, :], ALU.mult).then_inc(ring_free, 1)

                def negate_max(h, r):
                    eng.wait_ge(ring_free, r)
                    eng.tensor_reduce(m4[:, :], mx[:, :, :], AX.X, ALU.max).then_inc(max_step, 1)
                    eng.wait_ge(max_step, 2 * h + 1)
                    eng.tensor_scalar(nm[:, :, 0], m4[:, :], -1.0, None, ALU.mult).then_inc(max_step, 1)
                    eng.wait_ge(max_step, 2 * h + 2)
                    eng.scalar_tensor_tensor(out=nm[:, :, 1], in0=m4[:, :], scalar=-1.0,
                                             in1=nm[:, :, 0].bitcast(F32), op0=ALU.mult, op1=ALU.subtract)\
                       .then_inc(nm_ready, 1)

                def add(h, g):
                    tile = prob[:, (2 * g) % 4, 1, :]
                    if g == 0:
                        wait(eng, pv_done, NG * h)
                        return
                    eng.wait_ge(exp_done, h * 2 * NG + 2 * g + 1)
                    if g == 1:
                        eng.tensor_tensor(dve_sum[:, :], prob[:, 0, 1, :], tile, ALU.add).then_inc(dve_added, 2)
                    else:
                        eng.wait_ge(dve_added, h * (NG - 1) + g)
                        eng.tensor_tensor(dve_sum[:, :], dve_sum[:, :], tile, ALU.add).then_inc(dve_added, 1)

                def copy_out(h):
                    eng.wait_ge(pv_done, NG * h)
                    eng.tensor_copy(dsb[:, :], psum[:, DEN, :]).then_inc(od_out, 1)
                    eng.tensor_copy(osb[:, :], psum[:, OUT, :]).then_inc(od_out, 1)

                def step(i, u, first=False, last=False):
                    h = i * 2 + u
                    base = ring_base(h)
                    par = ring_base(2 + u) % 2
                    items = ring_items(h, first, last)
                    out_done = first
                    added = 0
                    for k, it in enumerate(items):
                        while added < min(it[0] - 1, NG - 1):
                            add(h, added)
                            added += 1
                        if it[0] == 1 and not out_done:
                            copy_out(h)
                            out_done = True
                        if it[1] == "neg":
                            negate_max(h + 1, base + k)
                        if it[1] in ("den", "sum"):
                            take(it, base + k, (par + k) % 2, h, 1 - u, i if u == 1 else i - 1)
                        else:
                            take(it, base + k, (par + k) % 2, h, 1 - u, i)
                    for g in range(added, NG - 1):
                        add(h, g)

                eng.wait_ge(nm_zero, 1)
                for n, (kc, qt) in enumerate([(k // TT, k % TT) for k in range(NCH * TT)]):
                    take((0, "max", kc, qt), n, n % 2, 0, 0, 0)
                negate_max(0, NCH * TT)
                take((0, "neg", 0, 0), NCH * TT, 0, 0, 0, 0)
                step(0, 0, first=True)
                step(0, 1)
                with eng.Fori(1, H // 2 - 1) as i:
                    step(i, 0)
                    step(i, 1)
                step(H // 2 - 1, 0)
                step(H // 2 - 1, 1, last=True)
                copy_out(H)
                end = ring_end
                take((0, "den", 0, 0), end, end % 2, H, 1, H // 2 - 1)
                take((0, "sum", 0, 0), end + 1, (end + 1) % 2, H, 1, H // 2 - 1)

        with ExitStack() as ctx:
            sb3 = alloc(ctx)
            xt = sb3("xt", [P, KT, T])
            raw = [sb3(f"raw{n}", [P, KT, D]) for n in range(2)]
            bh = [sb3(f"bh{n}", [P, KT, D], F32R) for n in range(4)]
            bl = [sb3(f"bl{n}", [P, KT, D], F32R) for n in range(4)]
            gate = sb3("gate", [P, KT, T])
            y = sb3("y", [P, KT, T])
            hf = sb3("hf", [P, KT, T])
            hh = [sb3(f"hh{n}", [P, KT, T], F32R) for n in range(2)]
            hl = [sb3(f"hl{n}", [P, KT, T], F32R) for n in range(2)]
            graw = sb3("graw", [P, KT, NEXP])
            gh = sb3("gh", [P, KT, NEXP], F32R)
            gl = sb3("gl", [P, KT, NEXP], F32R)
            ss = sb3("ss", [P, TT])
            pr = sb3("pr", [P, TT, NEXP])
            pe = sb3("pe", [P, TT, NEXP])
            r1 = sb3("r1", [P, TT])
            cmp_ = sb3("cmp", [P, TT, NEXP, NEXP])
            eq_ = sb3("eq", [P, TT, NEXP, NEXP])
            before = sb3("before", [P, NEXP, NEXP])
            rank = sb3("rank", [P, TT, NEXP])
            wt = sb3("wt", [P, TT, NEXP])

            s_att = sem("s_att")
            s_gw = sem("s_gw")
            s_raw = [sem(f"s_raw{n}") for n in range(2)]
            act_bh = sem("act_bh")
            pool_bl = sem("pool_bl")
            pe_out = sem("pe_out")
            act_ah = sem("act_ah")
            dve_al = sem("dve_al")
            act_gh = sem("act_gh")
            dve_gl = sem("dve_gl")
            dve_xs = sem("dve_xs")
            act_sig = sem("act_sig")
            dve_y = sem("dve_y")
            dve_qy = sem("dve_qy")
            dve_logits = sem("dve_logits")
            act_pe = sem("act_pe")
            act_sg = sem("act_sg")
            dve_gu = sem("dve_gu")
            act_hs = sem("act_hs")
            dve_hs = sem("dve_hs")
            dve_x3 = sem("dve_x3")
            tri = sem("tri")
            pe_h = sem("pe_h")
            pe_y = sem("pe_y")
            act_silu = sem("act_silu")
            act_hh = sem("act_hh")
            dve_hl = sem("dve_hl")
            dve_acc = sem("dve_acc")
            s_out = sem("s_out")

            NS = 7
            WE, WA, WKV, WQ, SG, SU, SD = range(NS)

            def slot(n):
                return n % 4

            W1 = (slot(NS), slot(NS + 1))
            W2 = (slot(NS + 2), slot(NS + 3))

            OUT_WE, OUT_A, OUT_KV, OUT_Q = TT, 2 * TT, 3 * TT, 4 * TT
            OUT_LOG, OUT_G, OUT_U, OUT_D = 4 * TT + 1, 5 * TT + 1, 6 * TT + 1, 7 * TT + 1
            last_use = (OUT_WE, OUT_A, OUT_KV, OUT_Q, OUT_G, OUT_U, OUT_D)

            block = ctx.enter_context(nc.Block())

            def split_load(eng, n, src, r):
                wait(eng, pool_bl, n - 1)
                eng.dma_start(raw[r][:, :, :], src).then_inc(s_raw[r], 16)

            def split_hi(eng, r, sl, use, used_by, count):
                eng.wait_ge(s_raw[r], 16 * use + 16)
                wait(eng, used_by, count)
                eng.activation(bh[sl][:, :, :], raw[r][:, :, :], ACT.Copy).then_inc(act_bh, 1)

            def split_lo(eng, n, r, sl):
                eng.wait_ge(act_bh, n + 1)
                eng.tensor_tensor(bl[sl][:, :, :], raw[r][:, :, :], bh[sl][:, :, :].bitcast(F32), ALU.subtract)\
                   .then_inc(pool_bl, 1)

            @block.sync
            def _(eng):
                eng.dma_start(xt[:, :, :], rows(att_d)).then_inc(s_att, 16)
                eng.dma_start(graw[:, :, :], rows(gate_wT)).then_inc(s_gw, 16)
                straight = [rows(we), rows(w_qkvaT)[:, :, 2 * D:3 * D], rows(w_qkvaT)[:, :, D:2 * D],
                            rows(w_qkvaT)[:, :, 0:D], rows(sguT)[:, :, 0:D], rows(sguT)[:, :, D:2 * D],
                            rows(sdownT), rows(w1T[0, :, :]), rows(w1T[1, :, :]), rows(w2T[0, :, :])]
                for n, src in enumerate(straight):
                    split_load(eng, n, src, n % 2)
                with eng.Fori(0, NEXP - 2) as e:
                    split_load(eng, e * 2 + NS + 3, rows(w1T[e + 2, :, :]), 0)
                    split_load(eng, e * 2 + NS + 4, rows(w2T[e + 1, :, :]), 1)
                split_load(eng, 2 * (NEXP - 2) + NS + 3, rows(w2T[NEXP - 1, :, :]), 0)
                eng.wait_ge(dve_acc, TT * NEXP)
                eng.dma_start(out.rearrange("(k p) n -> p k n", p=P), X[:, :, :]).then_inc(s_out, 16)
                eng.wait_ge(s_out, 16)

            @block.gpsimd
            def _(eng):
                eng.memset(before[:, :, :], 0.0).then_inc(tri, 1)
                eng.wait_ge(tri, 1)
                eng.affine_select(out=before[:, :, :], in_=before[:, :, :], compare_op=ALU.is_ge, fill=1.0, base=0,
                                  pattern=[[-1, NEXP], [1, NEXP]], channel_multiplier=0).then_inc(tri, 1)
                for n in range(NS + 3):
                    split_lo(eng, n, n % 2, slot(n))
                with eng.Fori(0, NEXP // 2 - 1) as i:
                    for u in range(2):
                        n = (i * 2 + u) * 2 + NS + 3
                        split_lo(eng, n, 0, W1[u])
                        split_lo(eng, n + 1, 1, W2[1 - u])
                split_lo(eng, 2 * (NEXP - 2) + NS + 3, 0, W2[1])

            @block.scalar
            def _(eng):
                def hi(n):
                    split_hi(eng, n % 2, slot(n), n // 2, pe_out, last_use[n - 4] if n >= 4 else 0)

                hi(0)
                eng.wait_ge(s_att, 16)
                eng.activation(AH[:, :, :], xt[:, :, :], ACT.Copy).then_inc(act_ah, 1)
                eng.wait_ge(s_gw, 16)
                eng.activation(gh[:, :, :], graw[:, :, :], ACT.Copy).then_inc(act_gh, 1)
                for n in (1, 2, 3):
                    hi(n)
                root_act(eng, 2)
                root_act(eng, 3)
                for k in range(KT):
                    eng.wait_ge(pe_tr, KT + k + 1)
                    eng.activation(AH[:, k, :], psum[:, k, :], ACT.Copy, scale=bcol[:, 2, k:k + 1]).then_inc(act_hi, 1)
                hi(4)
                for m in range(KT):
                    eng.wait_ge(pe_out, OUT_WE + m + 1)
                    eng.activation(gate[:, m, :], psum[:, m, :], ACT.Sigmoid).then_inc(act_sig, 1)
                for n in (5, 6, 7):
                    hi(n)
                root_act(eng, 4)
                for k in range(KT):
                    eng.wait_ge(pe_tr, 3 * KT + k + 1)
                    eng.activation(AH[:, k, :], psum[:, k, :], ACT.Copy).then_inc(act_hi, 1)
                eng.wait_ge(dve_logits, 1)
                eng.activation(pe[:, :, :], pr[:, :, :], ACT.Exp).then_inc(act_pe, 1)
                for m in range(KT):
                    eng.wait_ge(pe_out, OUT_LOG + m + 1)
                    eng.activation(gate[:, m, :], psum[:, m, :], ACT.Silu).then_inc(act_sg, 1)
                for m in range(KT):
                    eng.wait_ge(dve_gu, m + 1)
                    eng.activation(hh[0][:, m, :], y[:, m, :], ACT.Copy).then_inc(act_hs, 1)
                hi(8)
                hi(9)

                def silu(e, u):
                    wait(eng, dve_hl, KT * e)
                    wait(eng, pe_y, TT * (e - 1))
                    for m in range(KT):
                        eng.wait_ge(pe_h, KT * e + m + 1)
                        eng.activation(hf[:, m, :], psum[:, m, :], ACT.Silu).then_inc(act_silu, 1)
                    for m in range(KT):
                        eng.wait_ge(act_silu, KT * e + m + 1)
                        eng.activation(hh[u][:, m, :], hf[:, m, :], ACT.Copy).then_inc(act_hh, 1)

                silu(0, 0)

                def expert(e, u, w1=True):
                    if w1:
                        split_hi(eng, 0, W1[u], e + 5, pe_h, KT * (e + 1))
                    r = 1 if w1 else 0
                    if isinstance(e, int) and e == 0:
                        split_hi(eng, r, W2[1 - u], e + 5, pe_out, OUT_D)
                    else:
                        split_hi(eng, r, W2[1 - u], e + 5, pe_y, TT * e)
                    silu(e + 1, 1 - u)

                expert(0, 0)
                expert(1, 1)
                with eng.Fori(1, NEXP // 2 - 1) as i:
                    expert(i * 2, 0)
                    expert(i * 2 + 1, 1)
                expert(NEXP - 2, 0, w1=False)

            @block.tensor
            def _(eng):
                def weights(n):
                    eng.wait_ge(pool_bl, n + 1)
                    return bh[slot(n)], bl[slot(n)]

                eng.wait_ge(act_ah, 1)
                eng.wait_ge(dve_al, 1)
                h_, l_ = weights(WE)
                for t in range(TT):
                    product3(eng, psum[:, t, :], AH, AL, h_, l_, slice(t * P, (t + 1) * P)).then_inc(pe_out, 1)
                eng.wait_ge(dve_xs, TT)
                transpose_pe(eng)
                eng.wait_ge(act_hi, 2 * KT)
                eng.wait_ge(dve_lo, 2 * KT)
                for b, n in ((0, WA), (KT, WKV), (0, WQ)):
                    h_, l_ = weights(n)
                    for m in range(KT):
                        if n == WQ:
                            eng.wait_ge(act_sig, m + 1)
                        product3(eng, psum[:, b + m, :], h_, l_, AH, AL, slice(m * P, (m + 1) * P))\
                            .then_inc(pe_out, 1)
                eng.wait_ge(dve_qy, KT)
                for t in range(TT):
                    for k in range(KT):
                        ins = eng.transpose(psum[:, 4 + t, k * P:(k + 1) * P], y[:, k, t * P:(t + 1) * P], ident[:, :])
                    ins.then_inc(pe_tr, 1)
                eng.wait_ge(dve_xn, 3 * TT)
                transpose_pe(eng)
                eng.wait_ge(act_hi, 3 * KT)
                eng.wait_ge(dve_lo, 3 * KT)
                eng.wait_ge(act_gh, 1)
                eng.wait_ge(dve_gl, 1)
                for t in range(TT):
                    ins = product3(eng, psum[:, 4, t * NEXP:(t + 1) * NEXP], AH, AL, gh, gl, slice(t * P, (t + 1) * P))
                ins.then_inc(pe_out, 1)
                for b, n in ((0, SG), (KT, SU)):
                    h_, l_ = weights(n)
                    if n == SU:
                        eng.wait_ge(dve_logits, 1)
                    for m in range(KT):
                        product3(eng, psum[:, b + m, :], h_, l_, AH, AL, slice(m * P, (m + 1) * P))\
                            .then_inc(pe_out, 1)
                eng.wait_ge(act_hs, KT)
                eng.wait_ge(dve_hs, KT)
                h_, l_ = weights(SD)
                for t in range(TT):
                    product3(eng, psum[:, t, :], hh[0], hl[0], h_, l_, slice(t * P, (t + 1) * P)).then_inc(pe_out, 1)

                def first(e, u):
                    if isinstance(e, int) and e == 0:
                        eng.wait_ge(pool_bl, NS + 1)
                        eng.wait_ge(dve_x3, TT)
                    else:
                        eng.wait_ge(pool_bl, e * 2 + NS)
                    for m in range(KT):
                        wait(eng, act_silu, KT * (e - 1) + m + 1)
                        ins = product3(eng, psum[:, m, :], bh[W1[u]], bl[W1[u]], AH, AL, slice(m * P, (m + 1) * P))
                        ins.then_inc(pe_h, 1)

                def second(e, u, last=False):
                    eng.wait_ge(pool_bl, e * 2 + NS + 3 - (1 if last else 0))
                    eng.wait_ge(dve_hl, KT * (e + 1))
                    eng.wait_ge(act_hh, KT * (e + 1))
                    for t in range(TT):
                        wait(eng, dve_acc, TT * (e - 1) + t + 1)
                        ins = product3(eng, psum[:, 4 + t, :], hh[u], hl[u], bh[W2[u]], bl[W2[u]],
                                       slice(t * P, (t + 1) * P))
                        ins.then_inc(pe_y, 1)

                first(0, 0)

                def expert(e, u, last=False):
                    if not last:
                        first(e + 1, 1 - u)
                    second(e, u, last)

                expert(0, 0)
                expert(1, 1)
                with eng.Fori(1, NEXP // 2 - 1) as i:
                    expert(i * 2, 0)
                    expert(i * 2 + 1, 1)
                expert(NEXP - 2, 0)
                expert(NEXP - 1, 1, last=True)

            @block.vector
            def _(eng):
                for t in range(TT):
                    ins = eng.tensor_tensor(X[:, t, :], X[:, t, :], brow[:, 1, :], ALU.add)
                link(eng, ins)
                eng.wait_ge(act_ah, 1)
                eng.tensor_tensor(AL[:, :, :], xt[:, :, :], AH[:, :, :].bitcast(F32), ALU.subtract).then_inc(dve_al, 1)
                eng.wait_ge(act_gh, 1)
                eng.tensor_tensor(gl[:, :, :], graw[:, :, :], gh[:, :, :].bitcast(F32), ALU.subtract)\
                   .then_inc(dve_gl, 1)
                for t in range(TT):
                    eng.wait_ge(pe_out, t + 1)
                    ins = eng.tensor_tensor(X[:, t, :], X[:, t, :], psum[:, t, :], ALU.add)
                link(eng, ins)
                layer_norm_dve(eng)
                eng.wait_ge(dve_xn, 2 * TT)
                for t in range(TT):
                    ins = eng.tensor_tensor_reduce(y[:, t, :], XN[:, t, :], XN[:, t, :], 1.0, 0.0, ALU.mult, ALU.add,
                                                   ss[:, t:t + 1])
                link(eng, ins)
                eng.tensor_scalar(ve[:, :], ss[:, :], NORM_EPS * NORM_EPS, None, ALU.max).then_inc(dve_ve, 1)
                inverse_root_dve(eng)
                for t in range(TT):
                    eng.tensor_scalar(XN[:, t, :], XN[:, t, :], rs[:, t:t + 1], float(D) ** 0.5, ALU.mult, ALU.mult)\
                       .then_inc(dve_xs, 1)
                for k in range(KT):
                    eng.wait_ge(act_hi, KT + k + 1)
                    eng.scalar_tensor_tensor(out=AL[:, k, :], in0=psum[:, k, :], scalar=bcol[:, 2, k:k + 1],
                                             in1=AH[:, k, :].bitcast(F32), op0=ALU.mult, op1=ALU.subtract)\
                       .then_inc(dve_lo, 1)
                for m in range(KT):
                    eng.wait_ge(act_sig, m + 1)
                    eng.wait_ge(pe_out, OUT_A + m + 1)
                    eng.tensor_tensor_scan(y[:, m, :], gate[:, m, :], psum[:, KT + m, :], 0.0, ALU.mult, ALU.add)\
                       .then_inc(dve_y, 1)
                for m in range(KT):
                    eng.wait_ge(dve_y, m + 1)
                    eng.wait_ge(pe_out, OUT_KV + m + 1)
                    eng.tensor_tensor(y[:, m, :], y[:, m, :], psum[:, m, :], ALU.mult).then_inc(dve_qy, 1)
                for t in range(TT):
                    eng.wait_ge(pe_tr, 2 * KT + t + 1)
                    ins = eng.tensor_tensor(X[:, t, :], X[:, t, :], psum[:, 4 + t, :], ALU.add)
                link(eng, ins)
                layer_norm_dve(eng)
                for k in range(KT):
                    eng.wait_ge(act_hi, 2 * KT + k + 1)
                    eng.tensor_tensor(AL[:, k, :], psum[:, k, :], AH[:, k, :].bitcast(F32), ALU.subtract)\
                       .then_inc(dve_lo, 1)

                def over_experts(ap):
                    return ap.unsqueeze(2).to_broadcast([P, TT, NEXP])

                logits = psum[:, 4, 0:TT * NEXP].rearrange("p (t e) -> p t e", e=NEXP)
                eng.wait_ge(pe_out, OUT_LOG)
                link(eng, eng.tensor_reduce(r1[:, :], logits, AX.X, ALU.max))
                eng.tensor_tensor(pr[:, :, :], logits, over_experts(r1[:, :]), ALU.subtract).then_inc(dve_logits, 1)
                for m in range(KT):
                    eng.wait_ge(act_sg, m + 1)
                    eng.wait_ge(pe_out, OUT_G + m + 1)
                    eng.tensor_tensor(y[:, m, :], gate[:, m, :], psum[:, KT + m, :], ALU.mult).then_inc(dve_gu, 1)
                for m in range(KT):
                    eng.wait_ge(act_hs, m + 1)
                    eng.tensor_tensor(hl[0][:, m, :], y[:, m, :], hh[0][:, m, :].bitcast(F32), ALU.subtract)\
                       .then_inc(dve_hs, 1)
                eng.wait_ge(act_pe, 1)
                link(eng, eng.tensor_reduce(r1[:, :], pe[:, :, :], AX.X, ALU.add))
                link(eng, eng.reciprocal(t0[:, :], r1[:, :]))
                link(eng, eng.tensor_tensor(pr[:, :, :], pe[:, :, :], over_experts(t0[:, :]), ALU.mult))
                mine = pr[:, :, :].unsqueeze(3).to_broadcast([P, TT, NEXP, NEXP])
                other = pr[:, :, :].unsqueeze(2).to_broadcast([P, TT, NEXP, NEXP])
                link(eng, eng.tensor_tensor(cmp_[:, :, :, :], other, mine, ALU.is_gt))
                link(eng, eng.tensor_tensor(eq_[:, :, :, :], other, mine, ALU.is_equal))
                eng.wait_ge(tri, 2)
                link(eng, eng.tensor_tensor(eq_[:, :, :, :], eq_[:, :, :, :],
                                            before[:, :, :].unsqueeze(1).to_broadcast([P, TT, NEXP, NEXP]), ALU.mult))
                link(eng, eng.tensor_tensor(cmp_[:, :, :, :], cmp_[:, :, :, :], eq_[:, :, :, :], ALU.add))
                link(eng, eng.tensor_reduce(rank[:, :, :], cmp_[:, :, :, :], AX.X, ALU.add))
                link(eng, eng.tensor_scalar(rank[:, :, :], rank[:, :, :], float(TOPK), None, ALU.is_lt))
                link(eng, eng.tensor_tensor(wt[:, :, :], pr[:, :, :], rank[:, :, :], ALU.mult))
                link(eng, eng.tensor_reduce(r1[:, :], wt[:, :, :], AX.X, ALU.add))
                link(eng, eng.reciprocal(t0[:, :], r1[:, :]))
                link(eng, eng.tensor_tensor(wt[:, :, :], wt[:, :, :], over_experts(t0[:, :]), ALU.mult))
                for t in range(TT):
                    eng.wait_ge(pe_out, OUT_U + t + 1)
                    eng.tensor_tensor(X[:, t, :], X[:, t, :], psum[:, t, :], ALU.add).then_inc(dve_x3, 1)

                def split(e, u):
                    for m in range(KT):
                        eng.wait_ge(act_hh, KT * e + m + 1)
                        eng.tensor_tensor(hl[u][:, m, :], hf[:, m, :], hh[u][:, m, :].bitcast(F32), ALU.subtract)\
                           .then_inc(dve_hl, 1)

                def expert(e, u, last=False):
                    if not last:
                        split(e + 1, 1 - u)
                    for t in range(TT):
                        eng.wait_ge(pe_y, TT * e + t + 1)
                        if isinstance(e, int) and e == 0:
                            eng.wait_ge(dve_x3, t + 1)
                        else:
                            eng.wait_ge(dve_acc, TT * (e - 1) + t + 1)
                        eng.scalar_tensor_tensor(out=X[:, t, :], in0=psum[:, 4 + t, :],
                                                 scalar=wt[:, t, :][:, bass.ds(e, 1)], in1=X[:, t, :],
                                                 op0=ALU.mult, op1=ALU.add).then_inc(dve_acc, 1)

                split(0, 0)
                expert(0, 0)
                expert(1, 1)
                with eng.Fori(1, NEXP // 2 - 1) as i:
                    expert(i * 2, 0)
                    expert(i * 2 + 1, 1)
                expert(NEXP - 2, 0)
                expert(NEXP - 1, 1, last=True)


def kernel(**inputs):
    import numpy as np
    import concourse.bacc as bacc
    from concourse.bass_utils import run_bass_kernel_spmd

    def columns(v):
        return np.ascontiguousarray(np.asarray(v).reshape(KT, P).T)

    def transposed(a):
        return np.ascontiguousarray(np.swapaxes(np.asarray(a), -1, -2))

    laid_out = {
        "x": np.asarray(inputs["x"])[0],
        "ctxT": transposed(inputs["ctx_1024"])[0],
        "wq": inputs["L0_xattn_Wq"], "bq": columns(inputs["L0_xattn_bq"]),
        "wk": inputs["L0_xattn_Wk"], "bk": columns(inputs["L0_xattn_bk"]),
        "wv": inputs["L0_xattn_Wv"], "bv": np.asarray(inputs["L0_xattn_bv"]).reshape(1, D),
        "we": inputs["L0_xattn_We"], "be": np.asarray(inputs["L0_xattn_be"]).reshape(1, D),
        "w_qkvaT": transposed(inputs["L0_attn_W_qkva"]), "gamma": columns(inputs["L0_attn_gamma"]),
        "gate_wT": transposed(inputs["L0_ffn_gate_w"]),
        "w1T": transposed(inputs["L0_ffn_w1"]), "w2T": transposed(inputs["L0_ffn_w2"]),
        "sguT": transposed(inputs["L0_ffn_shared_gu"]), "sdownT": transposed(inputs["L0_ffn_shared_down"]),
    }
    nc = bacc.Bacc("TRN2", target_bir_lowering=False, num_devices=1)
    arrays, args = {}, []
    for name, a in laid_out.items():
        a = np.ascontiguousarray(a)
        arrays[name + "_dram"] = a
        args.append(nc.dram_tensor(name + "_dram", a.shape, mybir.dt.from_np(a.dtype), kind="ExternalInput").ap())
    args.append(nc.dram_tensor("out_dram", (T, D), F32, kind="ExternalOutput").ap())
    perceiver_program(nc, *args)
    r = run_bass_kernel_spmd(nc, [arrays], core_ids=[0])
    return np.asarray(r.results[0]["out_dram"]).reshape(1, T, D)
```

```python
from contextlib import ExitStack

import concourse.bass as bass
from concourse import mybir

F32 = mybir.dt.float32
F32R = mybir.dt.float32r
ALU = mybir.AluOpType
ACT = mybir.ActivationFunctionType
AX = mybir.AxisListType

P = 128
D = 512
KT = D // P
T = 512
TT = T // P
S = 8192
H = 16
E = D // H
CH = 512
NCH = S // CH
KEYT = S // P
NG = KEYT // 4
QUARTERS = 4
QK = S // QUARTERS
NEXP = 16
TOPK = 4
LN_EPS = 1e-5
NORM_EPS = 1e-12
SCALE = float(E) ** -0.5

PASS1_GROUPS = 14


PASS1 = [("max", k // TT, k % TT) for k in range(NCH * TT)]
RING = (5, 6, 7)
ITEMS = len(PASS1) + 2
SUM = 2 * len(PASS1) // PASS1_GROUPS

PAIRS = KEYT // 2
SLOTS = 6
POOL_PAIRS = KEYT // 3
POOL_ADDS = POOL_PAIRS - 1


def slot_of(u, p):
    return (p + SLOTS // 2 * u) % SLOTS


def slot_before(u, p):
    for back in range(1, 2 * SLOTS):
        q = p - back
        if q >= 0 and slot_of(u, q) == slot_of(u, p) or q < 0 and slot_of(1 - u, q + PAIRS) == slot_of(u, p):
            return back, q % PAIRS


def pool_adds(p):
    return max([1] + [t // 3 for t in (2 * p, 2 * p + 1) if t % 3])


def number(n):
    return n + 1 if n >= SUM else n


def schedule(first, last):
    out = []
    n = len(PASS1)
    for g in range(NG):
        mine = [] if last else [("item", number(k)) + PASS1[k] for k in
                                range(min(n, g * n // PASS1_GROUPS), min(n, (g + 1) * n // PASS1_GROUPS))]
        cuts = [mine[0:1], mine[1:2], mine[2:3], mine[3:]]
        if g == 1 and not first:
            cuts[3] = cuts[3] + [("item", SUM, "sum", 0, 0)]
        if g == NG - 1 and not last:
            cuts[1] = cuts[1] + [("item", ITEMS - 1, "neg", 0, 0)]
        for b in range(2):
            out.append(("st", g, b))
            out += cuts[2 * b]
            if g > 0 or not first:
                out.append(("pv", (g - 1) % NG, b))
            out += cuts[2 * b + 1]
    return out


def ring_at(h, k):
    bank, banks = k % len(RING), len(RING)
    missing = (h + 1 if isinstance(h, int) and h < 1 else 2)
    if isinstance(h, int) and h < 1 and k > SUM:
        missing += 1
    if isinstance(h, int) and h >= H - 1:
        return (H * ITEMS - 2 + h - (H - 1), H * (ITEMS // banks) - 2 + h - (H - 1), bank)
    return ((h + 1) * ITEMS + k - missing,
            (h + 1) * (ITEMS // banks) + k // banks - (missing if bank == SUM % banks else 0), bank)


def wait(eng, sem, value):
    if isinstance(value, int) and value <= 0:
        return
    eng.wait_ge(sem, value)


def perceiver_program(nc, x, ctxT, wq, bq, wk, bk, wv, bv, we, be, w_qkvaT, gamma, gate_wT, w1T, w2T,
                      sguT, sdownT, out):
    def rows(ap):
        return ap.rearrange("(k p) n -> p k n", p=P)

    kh_d = nc.dram_tensor("kh_scratch", (D, S), F32, kind="Internal").ap()
    kl_d = nc.dram_tensor("kl_scratch", (D, S), F32, kind="Internal").ap()
    qh_d = nc.dram_tensor("qh_scratch", (D, T), F32, kind="Internal").ap()
    ql_d = nc.dram_tensor("ql_scratch", (D, T), F32, kind="Internal").ap()
    v_d = nc.dram_tensor("v_scratch", (H, P, KEYT * E), F32, kind="Internal").ap()
    att_d = nc.dram_tensor("att_scratch", (D, T), F32, kind="Internal").ap()
    den_d = nc.dram_tensor("den_scratch", (D, T), F32, kind="Internal").ap()

    with ExitStack() as whole:
        def alloc(ctx):
            return (lambda name, shape, dt=F32: ctx.enter_context(nc.sbuf_tensor(name, shape, dt)))

        def sem(name):
            return whole.enter_context(nc.semaphore(name))

        sb = alloc(whole)
        psum = whole.enter_context(nc.psum_tensor("psum", [P, 8, 512], F32))

        X = sb("X", [P, TT, D])
        XN = sb("XN", [P, TT, D])
        AH = sb("AH", [P, KT, T], F32R)
        AL = sb("AL", [P, KT, T], F32R)
        ident = sb("ident", [P, P])
        stats = sb("stats", [P, TT, 6])
        mv = sb("mv", [P, TT, 2])
        ve = sb("ve", [P, TT])
        sd = sb("sd", [P, TT])
        rs = sb("rs", [P, TT])
        t0 = sb("t0", [P, TT])
        bcol = sb("bcol", [P, 3, KT])
        brow = sb("brow", [P, 2, D])

        s_ident = sem("s_ident")
        s_x = sem("s_x")
        s_small = sem("s_small")
        dve_step = sem("dve_step")
        dve_ve = sem("dve_ve")
        act_sqrt = sem("act_sqrt")
        pe_tr = sem("pe_tr")
        act_hi = sem("act_hi")
        dve_lo = sem("dve_lo")
        dve_xn = sem("dve_xn")

        steps = [0]

        def link(eng, ins):
            steps[0] += 1
            ins.then_inc(dve_step, 1)
            eng.wait_ge(dve_step, steps[0])

        roots = [0]

        def inverse_root_dve(eng):
            roots[0] += 1
            eng.wait_ge(act_sqrt, roots[0])
            link(eng, eng.reciprocal(t0[:, :], sd[:, :]))
            link(eng, eng.tensor_tensor(t0[:, :], t0[:, :], ve[:, :], ALU.mult))
            link(eng, eng.tensor_tensor(t0[:, :], t0[:, :], sd[:, :], ALU.add))
            link(eng, eng.tensor_scalar(t0[:, :], t0[:, :], 0.5, None, ALU.mult))
            link(eng, eng.reciprocal(rs[:, :], t0[:, :]))

        def layer_norm_dve(eng):
            for t in range(TT):
                ins = eng.bn_stats(stats[:, t, :], X[:, t, :])
            link(eng, ins)
            for t in range(TT):
                ins = eng.bn_aggr(mv[:, t, :], stats[:, t, :])
            link(eng, ins)
            eng.tensor_scalar(ve[:, :], mv[:, :, 1], LN_EPS, None, ALU.add).then_inc(dve_ve, 1)
            inverse_root_dve(eng)
            for t in range(TT):
                eng.tensor_scalar(XN[:, t, :], X[:, t, :], mv[:, t, 0:1], rs[:, t:t + 1],
                                  ALU.subtract, ALU.mult).then_inc(dve_xn, 1)

        def root_act(eng, n):
            eng.wait_ge(dve_ve, n)
            eng.activation(sd[:, :], ve[:, :], ACT.Sqrt).then_inc(act_sqrt, 1)

        def transpose_pe(eng, first_bank=0):
            for k in range(KT):
                for t in range(TT):
                    ins = eng.transpose(psum[:, first_bank + k, t * P:(t + 1) * P], XN[:, t, k * P:(k + 1) * P],
                                        ident[:, :])
                ins.then_inc(pe_tr, 1)

        def product3(eng, bank_ap, lh, ll, rh, rl, m=None):
            n = 0
            for k in range(KT):
                for left, right in ((lh, rh), (lh, rl), (ll, rh)):
                    ins = eng.matmul(bank_ap, left[:, k, m], right[:, k, :], start=(n == 0), stop=(n == 3 * KT - 1))
                    n += 1
            return ins

        with ExitStack() as ctx:
            sb1 = alloc(ctx)
            wraw = sb1("wraw", [P, 3, KT, D])
            wh = sb1("wh", [P, 3, KT, D], F32R)
            wl = sb1("wl", [P, 3, KT, D], F32R)
            craw = sb1("craw", [P, 2, KT, CH])
            chi = sb1("chi", [P, 2, KT, CH], F32R)
            clo = sb1("clo", [P, 2, KT, CH], F32R)
            q32 = craw[:, 0, :, :]
            khi = sb1("khi", [P, KT, CH], F32R)
            klo = sb1("klo", [P, KT, CH], F32R)
            vsb = sb1("vsb", [P, H, 4, E])

            s_w = [sem(f"s_w{n}") for n in range(3)]
            act_wh = sem("act_wh")
            pool_wl = sem("pool_wl")
            pe_q = sem("pe_q")
            dve_q = sem("dve_q")
            dve_ql = sem("dve_ql")
            act_qh = sem("act_qh")
            s_qst = sem("s_qst")
            s_c = [sem(f"s_c{n}") for n in range(2)]
            act_ch = sem("act_ch")
            dve_cl = sem("dve_cl")
            pe_k = sem("pe_k")
            pe_v = sem("pe_v")
            act_kh = sem("act_kh")
            dve_kl = sem("dve_kl")
            dve_v = sem("dve_v")
            s_kst = sem("s_kst")
            s_vst = sem("s_vst")

            block = ctx.enter_context(nc.Block())

            @block.sync
            def _(eng):
                eng.dma_start(X[:, :, :], x.rearrange("(k p) n -> p k n", p=P)).then_inc(s_x, 16)
                for n, w in enumerate((wq, wk, wv)):
                    eng.dma_start(wraw[:, n, :, :], rows(w)).then_inc(s_w[n], 16)
                eng.dma_start(bcol[:, 0, :], bq).then_inc(s_small, 16)
                eng.dma_start(bcol[:, 1, :], bk).then_inc(s_small, 16)
                eng.dma_start(bcol[:, 2, :], gamma).then_inc(s_small, 16)
                eng.dma_start(brow[:, 0, :], bv.to_broadcast([P, D])).then_inc(s_small, 16)
                eng.dma_start(brow[:, 1, :], be.to_broadcast([P, D])).then_inc(s_small, 16)

                eng.dma_start(craw[:, 1, :, :], rows(ctxT)[:, :, CH:2 * CH]).then_inc(s_c[1], 16)
                eng.wait_ge(act_qh, KT)
                eng.wait_ge(dve_ql, KT)
                eng.dma_start(craw[:, 0, :, :], rows(ctxT)[:, :, 0:CH]).then_inc(s_c[0], 16)
                with eng.Fori(1, NCH // 2) as i:
                    for u in range(2):
                        eng.wait_ge(dve_cl, i * 2 + u - 1)
                        eng.dma_start(craw[:, u, :, :], rows(ctxT)[:, :, bass.ds((i * 2 + u) * CH, CH)])\
                           .then_inc(s_c[u], 16)

            @block.gpsimd
            def _(eng):
                eng.memset(ident[:, :], 0.0).then_inc(s_ident, 1)
                eng.wait_ge(s_ident, 1)
                eng.affine_select(out=ident[:, :], in_=ident[:, :], compare_op=ALU.not_equal, fill=1.0, base=0,
                                  pattern=[[-1, P]], channel_multiplier=1).then_inc(s_ident, 1)
                for n in range(3):
                    eng.wait_ge(act_wh, n + 1)
                    eng.tensor_tensor(wl[:, n, :, :], wraw[:, n, :, :], wh[:, n, :, :].bitcast(F32), ALU.subtract)\
                       .then_inc(pool_wl, 1)

            @block.scalar
            def _(eng):
                for n in range(3):
                    eng.wait_ge(s_w[n], 16)
                    eng.activation(wh[:, n, :, :], wraw[:, n, :, :], ACT.Copy).then_inc(act_wh, 1)
                root_act(eng, 1)
                for k in range(KT):
                    eng.wait_ge(pe_tr, k + 1)
                    eng.activation(AH[:, k, :], psum[:, k, :], ACT.Copy).then_inc(act_hi, 1)
                for m in range(KT):
                    eng.wait_ge(dve_q, m + 1)
                    eng.activation(chi[:, 0, m, :], q32[:, m, :], ACT.Copy).then_inc(act_qh, 1)
                eng.wait_ge(act_qh, KT)
                eng.dma_start(rows(qh_d), chi[:, 0, :, :].bitcast(F32)).then_inc(s_qst, 16)
                eng.wait_ge(dve_ql, KT)
                eng.dma_start(rows(ql_d), clo[:, 0, :, :].bitcast(F32)).then_inc(s_qst, 16)
                eng.wait_ge(s_qst, 32)

                def split(i, u):
                    c = i * 2 + u
                    eng.wait_ge(s_c[u], 16 * i + 16)
                    wait(eng, pe_v, 4 * (c - 1))
                    eng.activation(chi[:, u, :, :], craw[:, u, :, :], ACT.Copy).then_inc(act_ch, 1)

                def chunk(i, u, last=False):
                    c = i * 2 + u
                    if not last:
                        split(i + u, 1 - u)
                    wait(eng, s_kst, 32 * c)
                    for m in range(KT):
                        eng.wait_ge(pe_k, 4 * c + m + 1)
                        eng.activation(khi[:, m, :], psum[:, m, :], ACT.Identity, bias=bcol[:, 1, m:m + 1])\
                           .then_inc(act_kh, 1)
                    cols = bass.ds(c * CH, CH)
                    eng.wait_ge(act_kh, 4 * c + 4)
                    eng.dma_start(rows(kh_d)[:, :, cols], khi[:, :, :].bitcast(F32)).then_inc(s_kst, 16)
                    eng.wait_ge(dve_kl, 4 * c + 4)
                    eng.dma_start(rows(kl_d)[:, :, cols], klo[:, :, :].bitcast(F32)).then_inc(s_kst, 16)
                    eng.wait_ge(dve_v, 4 * c + 4)
                    eng.dma_start(v_d.rearrange("h p n -> p h n")[:, :, bass.ds(c * 4 * E, 4 * E)],
                                  vsb[:, :, :, :].rearrange("p h t e -> p h (t e)")).then_inc(s_vst, 16)

                split(0, 0)
                chunk(0, 0)
                chunk(0, 1)
                with eng.Fori(1, NCH // 2 - 1) as i:
                    chunk(i, 0)
                    chunk(i, 1)
                chunk(NCH // 2 - 1, 0)
                chunk(NCH // 2 - 1, 1, last=True)
                eng.wait_ge(s_kst, 32 * NCH)
                eng.wait_ge(s_vst, 16 * NCH)

            @block.tensor
            def _(eng):
                eng.wait_ge(s_ident, 2)
                eng.wait_ge(dve_xn, TT)
                transpose_pe(eng)
                eng.wait_ge(act_hi, KT)
                eng.wait_ge(dve_lo, KT)
                eng.wait_ge(act_wh, 1)
                eng.wait_ge(pool_wl, 1)
                for m in range(KT):
                    product3(eng, psum[:, 4 + m, :], wh[:, 0, :, :], wl[:, 0, :, :], AH, AL,
                             slice(m * P, (m + 1) * P)).then_inc(pe_q, 1)
                eng.wait_ge(act_wh, 3)
                eng.wait_ge(pool_wl, 3)

                def chunk(i, u):
                    c = i * 2 + u
                    eng.wait_ge(act_ch, c + 1)
                    eng.wait_ge(dve_cl, c + 1)
                    ch, cl = chi[:, u, :, :], clo[:, u, :, :]
                    for m in range(KT):
                        wait(eng, dve_kl, 4 * (c - 1) + m + 1)
                        product3(eng, psum[:, m, :], wh[:, 1, :, :], wl[:, 1, :, :], ch, cl,
                                 slice(m * P, (m + 1) * P)).then_inc(pe_k, 1)
                    for t in range(4):
                        if isinstance(c, int) and c == 0:
                            eng.wait_ge(dve_q, KT)
                        wait(eng, dve_v, 4 * (c - 1) + t + 1)
                        product3(eng, psum[:, 4 + t, :], ch, cl, wh[:, 2, :, :], wl[:, 2, :, :],
                                 slice(t * P, (t + 1) * P)).then_inc(pe_v, 1)

                chunk(0, 0)
                chunk(0, 1)
                with eng.Fori(1, NCH // 2) as i:
                    chunk(i, 0)
                    chunk(i, 1)

            @block.vector
            def _(eng):
                eng.wait_ge(s_x, 16)
                layer_norm_dve(eng)
                for k in range(KT):
                    eng.wait_ge(act_hi, k + 1)
                    eng.tensor_tensor(AL[:, k, :], psum[:, k, :], AH[:, k, :].bitcast(F32), ALU.subtract)\
                       .then_inc(dve_lo, 1)
                eng.wait_ge(s_small, 16 * 5)
                for m in range(KT):
                    eng.wait_ge(pe_q, m + 1)
                    eng.tensor_scalar(q32[:, m, :], psum[:, 4 + m, :], bcol[:, 0, m:m + 1], SCALE,
                                      ALU.add, ALU.mult).then_inc(dve_q, 1)
                for m in range(KT):
                    eng.wait_ge(act_qh, m + 1)
                    eng.tensor_tensor(clo[:, 0, m, :], q32[:, m, :], chi[:, 0, m, :].bitcast(F32), ALU.subtract)\
                       .then_inc(dve_ql, 1)
                eng.wait_ge(s_qst, 32)

                def split(c, u):
                    eng.wait_ge(act_ch, c + 1)
                    eng.tensor_tensor(clo[:, u, :, :], craw[:, u, :, :], chi[:, u, :, :].bitcast(F32), ALU.subtract)\
                       .then_inc(dve_cl, 1)

                def chunk(i, u, last=False):
                    c = i * 2 + u
                    if not last:
                        split(c + 1, 1 - u)
                    for m in range(KT):
                        eng.wait_ge(act_kh, 4 * c + m + 1)
                        eng.scalar_tensor_tensor(out=klo[:, m, :], in0=psum[:, m, :], scalar=bcol[:, 1, m:m + 1],
                                                 in1=khi[:, m, :].bitcast(F32), op0=ALU.add, op1=ALU.subtract)\
                           .then_inc(dve_kl, 1)
                    wait(eng, s_vst, 16 * c)
                    for t in range(4):
                        eng.wait_ge(pe_v, 4 * c + t + 1)
                        eng.tensor_tensor(vsb[:, :, t, :], psum[:, 4 + t, :].rearrange("p (h e) -> p h e", e=E),
                                          brow[:, 0, :].rearrange("p (h e) -> p h e", e=E), ALU.add)\
                           .then_inc(dve_v, 1)

                split(0, 0)
                chunk(0, 0)
                chunk(0, 1)
                with eng.Fori(1, NCH // 2 - 1) as i:
                    chunk(i, 0)
                    chunk(i, 1)
                chunk(NCH // 2 - 1, 0)
                chunk(NCH // 2 - 1, 1, last=True)

        with ExitStack() as ctx:
            sb2 = alloc(ctx)
            ks = [sb2(f"ks{n}", [P, S], F32R) for n in range(2)]
            qmax = [sb2(f"qmax{n}", [P, T], F32R) for n in range(2)]
            qexp = [sb2(f"qexp{n}", [P, T], F32R) for n in range(2)]
            vh = [sb2(f"vh{n}", [P, KEYT, E]) for n in range(2)]
            prob = sb2("prob", [P, 2 * SLOTS, T])
            pool_sum = [sb2(f"pool_sum{n}", [P, 2, T]) for n in range(2)]
            ones = sb2("ones", [P, E])
            sel = sb2("sel", [P, 2 * E])
            mx = sb2("mx", [P, TT, NCH])
            m4 = sb2("m4", [P, TT])
            nm = sb2("nm", [P, TT, E], F32R)
            osb = sb2("osb", [P, T])
            att = [sb2(f"att{n}", [2 * E, T]) for n in range(2)]

            const_c = sem("const_c")
            s_kq = [[sem(f"s_k{n}q{q}") for q in range(QUARTERS)] for n in range(2)]
            s_q1 = [sem(f"s_q1_{n}") for n in range(2)]
            s_q2 = [sem(f"s_q2_{n}") for n in range(2)]
            s_vh = [sem(f"s_vh{n}") for n in range(2)]
            st_ready = sem("st_ready")
            exp_done = sem("exp_done")
            pv_done = sem("pv_done")
            pool_added = sem("pool_added")
            ring_ready = sem("ring_ready")
            ring_free = [sem(f"ring_free{n}") for n in range(len(RING))]
            nm_zero = sem("nm_zero")
            nm_ready = sem("nm_ready")
            max_step = sem("max_step")
            sums_out = sem("sums_out")
            s_attst = [sem(f"s_attst{n}") for n in range(2)]

            def taken(eng, at):
                eng.wait_ge(ring_free[at[2]], at[1] + 1)

            OUT = 4

            block = ctx.enter_context(nc.Block())

            def head_rows(ap, h):
                return ap[bass.ds(h * E, E), :]

            @block.sync
            def _(eng):
                def load_quarter(h, n, q):
                    cols = slice(q * QK, (q + 1) * QK)
                    for part, src in enumerate((kh_d, kh_d, kl_d)):
                        eng.dma_start(ks[n][part * E:(part + 1) * E, cols].bitcast(F32), head_rows(src, h)[:, cols])\
                           .then_inc(s_kq[n][q], 16)

                def load_q(h, tile, s):
                    for part, src in enumerate((qh_d, ql_d, qh_d)):
                        eng.dma_start(tile[part * E:(part + 1) * E, :].bitcast(F32), head_rows(src, h))\
                           .then_inc(s, 16)

                def load_v(h, n):
                    eng.dma_start(vh[n][:, :, :].rearrange("p t e -> p (t e)"), v_d[h, :, :]).then_inc(s_vh[n], 16)

                load_q(0, qmax[0], s_q1[0])
                for q in range(QUARTERS):
                    load_quarter(0, 0, q)
                load_q(0, qexp[0], s_q2[0])
                load_v(0, 0)
                load_q(1, qmax[1], s_q1[1])
                for q in range(QUARTERS):
                    load_quarter(1, 1, q)

                def store(h, u, uses=None):
                    taken(eng, ring_at(h + 1, SUM))
                    eng.dma_start(head_rows(att_d, h), att[u][0:E, :]).then_inc(s_attst[u], 16)
                    eng.dma_start(head_rows(den_d, h), att[u][E:2 * E, :]).then_inc(s_attst[u], 16)

                def step(i, u, first=False, has_next=True, has_next2=True):
                    h = i * 2 + u
                    if has_next2:
                        eng.wait_ge(nm_ready, h + 1)
                        load_q(h + 2, qmax[u], s_q1[u])
                    if has_next:
                        wait(eng, pv_done, PAIRS * h)
                        load_q(h + 1, qexp[1 - u], s_q2[1 - u])
                        load_v(h + 1, 1 - u)
                    if not first:
                        store(h - 1, 1 - u)
                    if has_next2:
                        for q in range(QUARTERS):
                            eng.wait_ge(st_ready, PAIRS * h + PAIRS // QUARTERS * (q + 1))
                            load_quarter(h + 2, u, q)

                step(0, 0, first=True)
                step(0, 1)
                with eng.Fori(1, H // 2 - 1) as i:
                    step(i, 0)
                    step(i, 1)
                step(H // 2 - 1, 0, has_next2=False)
                step(H // 2 - 1, 1, has_next=False, has_next2=False)
                store(H - 1, 1)
                for n in range(2):
                    eng.wait_ge(s_attst[n], 16 + 32 * H // 2)

            @block.gpsimd
            def _(eng):
                for n in range(2):
                    eng.memset(ks[n][3 * E:P, :].bitcast(F32), 0.0).then_inc(const_c, 1)
                    eng.wait_ge(const_c, 2 * n + 1)
                    eng.memset(ks[n][3 * E:3 * E + 2, :].bitcast(F32), 1.0).then_inc(const_c, 1)
                    eng.wait_ge(const_c, 2 * n + 2)
                eng.memset(ones[:, :], 1.0).then_inc(const_c, 1)
                eng.memset(sel[:, :], 0.0).then_inc(const_c, 1)
                for j in range(4):
                    half = sel[:, j // 3 * E:(j // 3 + 1) * E]
                    eng.wait_ge(const_c, 6 + j)
                    eng.affine_select(out=half, in_=half, compare_op=ALU.not_equal, fill=1.0,
                                      base=-E * j, pattern=[[-1, E]], channel_multiplier=1).then_inc(const_c, 1)

                def step(h, u, use_over=True):
                    for k in range(1, POOL_PAIRS):
                        if k == 1 and use_over:
                            taken(eng, ring_at(h - 1, SUM))
                        eng.wait_ge(exp_done, h * PAIRS + (3 * k + 2) // 2 + 1)
                        tiles = [(3 * n + 1 + SLOTS * u) % (2 * SLOTS) for n in (0, k)]
                        pair = prob[:, tiles[1]:tiles[1] + 2, :]
                        if k == 1:
                            so_far = prob[:, tiles[0]:tiles[0] + 2, :]
                        else:
                            so_far = pool_sum[u][:, :, :]
                            eng.wait_ge(pool_added, h * POOL_ADDS + k - 1)
                        eng.tensor_tensor(pool_sum[u][:, :, :], so_far, pair, ALU.add).then_inc(pool_added, 1)

                step(0, 0, use_over=False)
                step(1, 1, use_over=False)
                with eng.Fori(1, H // 2) as i:
                    step(i * 2, 0)
                    step(i * 2 + 1, 1)

            @block.scalar
            def _(eng):
                def copy_out(h):
                    eng.wait_ge(pv_done, PAIRS * (h + 1))
                    eng.activation(osb[:, :], psum[:, OUT, :], ACT.Copy).then_inc(sums_out, 1)

                def step(h, u, first=False):
                    for p in range(PAIRS):
                        eng.wait_ge(st_ready, h * PAIRS + p + 1)
                        back, q = slot_before(u, p)
                        wait(eng, pv_done, h * PAIRS + p - back + 1)
                        if not (first and back > p):
                            eng.wait_ge(pool_added, (h * POOL_ADDS - (POOL_ADDS if back > p else 0)) + pool_adds(q))
                        at, b = 2 * slot_of(u, p), p % 2
                        eng.activation(prob[:, at:at + 2, :], psum[:, 2 * b:2 * b + 2, :], ACT.Exp).then_inc(exp_done, 1)
                        if p == 1 and not first:
                            copy_out(h - 1)

                step(0, 0, first=True)
                step(1, 1)
                with eng.Fori(1, H // 2) as i:
                    step(i * 2, 0)
                    step(i * 2 + 1, 1)
                copy_out(H - 1)

            @block.tensor
            def _(eng):
                def item(e, at, n, use=None, h=None):
                    _, _, kind, kc, qt = e
                    quarter, rest = divmod(kc, NCH // QUARTERS)
                    if kind == "max" and qt == 0 and rest == 0:
                        if quarter == 0:
                            eng.wait_ge(s_q1[n], 48 * use + 48)
                        eng.wait_ge(s_kq[n][quarter], 48 * use + 48)
                    if kind == "neg":
                        eng.wait_ge(nm_ready, h + 2)
                    if kind == "sum":
                        eng.wait_ge(sums_out, h)
                        eng.wait_ge(pool_added, h * POOL_ADDS)
                    bank = RING[at[2]]
                    wait(eng, ring_free[at[2]], at[1])
                    if kind == "neg":
                        for t in range(TT):
                            ins = eng.matmul(psum[3 * E:P, bank, t * P:(t + 1) * P], nm[:, t, :].bitcast(F32),
                                             ident[:, :], start=True, stop=True, tile_position=(0, 3 * E))
                    elif kind == "sum":
                        for j in range(2):
                            eng.matmul(psum[j * E:(j + 1) * E, bank, :], sel[:, j * E:(j + 1) * E], osb[:, :],
                                       start=True, stop=(j == 0), tile_position=(0, j * E))
                        for t in range(2):
                            ins = eng.matmul(psum[E:2 * E, bank, :], ones[:, :], pool_sum[n][:, t, :],
                                             start=False, stop=(t == 1), tile_position=(0, E))
                    else:
                        ins = eng.matmul(psum[:, bank, :], qmax[n][0:3 * E, qt * P:(qt + 1) * P],
                                         ks[n][0:3 * E, kc * CH:(kc + 1) * CH], start=True, stop=True)
                    ins.then_inc(ring_ready, 1)

                def summed(h, u, g, b):
                    p = 2 * g + b
                    eng.wait_ge(exp_done, h * PAIRS + p + 1)
                    for n in (2 * p, 2 * p + 1):
                        tile = prob[:, 2 * slot_of(u, p) + n % 2, :]
                        shares = [(n % 3, vh[u][:, n, :], n < 3, n >= KEYT - 3)]
                        if n % 3 == 0:
                            shares.append((3, ones[:, :], n == 0, n == KEYT - 1))
                        for j, left, start, stop in shares:
                            ins = eng.matmul(psum[j * E:(j + 1) * E, OUT, :], left, tile, start=start, stop=stop,
                                             tile_position=(0, j * E))
                    ins.then_inc(pv_done, 1)

                def step(i, u, first=False, last=False):
                    h = i * 2 + u
                    eng.wait_ge(s_q2[u], 48 * i + 48)
                    eng.wait_ge(s_vh[u], 16 * i + 16)
                    taken(eng, ring_at(-1 if first else h - 1, ITEMS - 1))
                    for e in schedule(first, last):
                        if e[0] == "st":
                            _, g, b = e
                            wait(eng, exp_done, h * PAIRS + 2 * g + b - 1)
                            for t in range(2):
                                key = (4 * g + 2 * b + t) * P
                                ins = eng.matmul(psum[:, 2 * b + t, :], ks[u][:, key:key + P], qexp[u][:, :],
                                                 start=True, stop=True)
                            ins.then_inc(st_ready, 1)
                        elif e[0] == "pv":
                            _, g, b = e
                            if g == NG - 1:
                                summed(h - 1, 1 - u, g, b)
                            else:
                                if g == 0 and b == 0:
                                    wait(eng, sums_out, h)
                                summed(h, u, g, b)
                        else:
                            item(e, ring_at(h, e[1]), 1 - u, i + u, h)

                eng.wait_ge(const_c, 10)
                for k, it in enumerate(PASS1):
                    item(("item", number(k)) + it, ring_at(-1, number(k)), 0, 0, -1)
                item(("item", ITEMS - 1, "neg", 0, 0), ring_at(-1, ITEMS - 1), 0, h=-1)
                step(0, 0, first=True)
                step(0, 1)
                with eng.Fori(1, H // 2 - 1) as i:
                    step(i, 0)
                    step(i, 1)
                step(H // 2 - 1, 0)
                step(H // 2 - 1, 1, last=True)
                summed(H - 1, 1, NG - 1, 0)
                summed(H - 1, 1, NG - 1, 1)
                item(("item", SUM, "sum", 0, 0), ring_at(H, SUM), 1, h=H)

            @block.vector
            def _(eng):
                eng.memset(nm[:, :, :].bitcast(F32), 0.0).then_inc(nm_zero, 1)
                for n in range(2):
                    eng.memset(att[n][:, :], 0.0).then_inc(s_attst[n], 16)

                def take(e, at, n, stores=None):
                    _, _, kind, kc, qt = e
                    src = psum[:, RING[at[2]], :]
                    eng.wait_ge(ring_ready, at[0] + 1)
                    if kind == "max":
                        ins = eng.tensor_reduce(mx[:, qt, kc:kc + 1], src, AX.X, ALU.max)
                    elif kind == "neg":
                        ins = eng.tensor_copy(qexp[n][3 * E:P, :], psum[3 * E:P, RING[at[2]], :])
                    else:
                        eng.wait_ge(s_attst[n], 32 * stores + 16)
                        ins = eng.tensor_copy(att[n][:, :], src[0:2 * E, :])
                    ins.then_inc(ring_free[at[2]], 1)

                def negate_max(h):
                    for k in range(len(RING)):
                        taken(eng, ring_at(h - 1, ITEMS - 2 - k))
                    eng.tensor_reduce(m4[:, :], mx[:, :, :], AX.X, ALU.max).then_inc(max_step, 1)
                    eng.wait_ge(max_step, 2 * h + 1)
                    eng.tensor_scalar(nm[:, :, 0], m4[:, :], -1.0, None, ALU.mult).then_inc(max_step, 1)
                    eng.wait_ge(max_step, 2 * h + 2)
                    eng.scalar_tensor_tensor(out=nm[:, :, 1], in0=m4[:, :], scalar=-1.0,
                                             in1=nm[:, :, 0].bitcast(F32), op0=ALU.mult, op1=ALU.subtract)\
                       .then_inc(nm_ready, 1)

                def step(i, u, first=False, last=False):
                    h = i * 2 + u
                    for e in schedule(first, last):
                        if e[0] == "item":
                            if e[2] == "neg":
                                negate_max(h + 1)
                            take(e, ring_at(h, e[1]), 1 - u, i + u - 1)

                eng.wait_ge(nm_zero, 1)
                for k, it in enumerate(PASS1):
                    take(("item", number(k)) + it, ring_at(-1, number(k)), 0)
                negate_max(0)
                take(("item", ITEMS - 1, "neg", 0, 0), ring_at(-1, ITEMS - 1), 0)
                step(0, 0, first=True)
                step(0, 1)
                with eng.Fori(1, H // 2 - 1) as i:
                    step(i, 0)
                    step(i, 1)
                step(H // 2 - 1, 0)
                step(H // 2 - 1, 1, last=True)
                take(("item", SUM, "sum", 0, 0), ring_at(H, SUM), 1, H // 2 - 1)

        with ExitStack() as ctx:
            sb3 = alloc(ctx)
            xt = sb3("xt", [P, KT, T])
            raw = [sb3(f"raw{n}", [P, KT, D]) for n in range(2)]
            bh = [sb3(f"bh{n}", [P, KT, D], F32R) for n in range(4)]
            bl = [sb3(f"bl{n}", [P, KT, D], F32R) for n in range(4)]
            gate = sb3("gate", [P, KT, T])
            y = sb3("y", [P, KT, T])
            hf = sb3("hf", [P, KT, T])
            hh = [sb3(f"hh{n}", [P, KT, T], F32R) for n in range(2)]
            hl = [sb3(f"hl{n}", [P, KT, T], F32R) for n in range(2)]
            graw = sb3("graw", [P, KT, NEXP])
            gh = sb3("gh", [P, KT, NEXP], F32R)
            gl = sb3("gl", [P, KT, NEXP], F32R)
            ss = sb3("ss", [P, TT])
            pr = sb3("pr", [P, TT, NEXP])
            pe = sb3("pe", [P, TT, NEXP])
            r1 = sb3("r1", [P, TT])
            cmp_ = sb3("cmp", [P, TT, NEXP, NEXP])
            eq_ = sb3("eq", [P, TT, NEXP, NEXP])
            before = sb3("before", [P, NEXP, NEXP])
            rank = sb3("rank", [P, TT, NEXP])
            wt = sb3("wt", [P, TT, NEXP])

            xd = y

            s_att = sem("s_att")
            dve_xd = sem("dve_xd")
            dve_xt = sem("dve_xt")
            s_gw = sem("s_gw")
            s_raw = [sem(f"s_raw{n}") for n in range(2)]
            act_bh = sem("act_bh")
            pool_bl = sem("pool_bl")
            pe_out = sem("pe_out")
            act_ah = sem("act_ah")
            dve_al = sem("dve_al")
            act_gh = sem("act_gh")
            dve_gl = sem("dve_gl")
            dve_xs = sem("dve_xs")
            act_sig = sem("act_sig")
            dve_y = sem("dve_y")
            dve_qy = sem("dve_qy")
            dve_logits = sem("dve_logits")
            act_pe = sem("act_pe")
            act_sg = sem("act_sg")
            dve_gu = sem("dve_gu")
            act_hs = sem("act_hs")
            dve_hs = sem("dve_hs")
            dve_x3 = sem("dve_x3")
            tri = sem("tri")
            pe_h = sem("pe_h")
            pe_y = sem("pe_y")
            act_silu = sem("act_silu")
            act_hh = sem("act_hh")
            dve_hl = sem("dve_hl")
            dve_acc = sem("dve_acc")
            s_out = sem("s_out")

            NS = 7
            WE, WA, WKV, WQ, SG, SU, SD = range(NS)

            def slot(n):
                return n % 4

            W1 = (slot(NS), slot(NS + 1))
            W2 = (slot(NS + 2), slot(NS + 3))

            OUT_WE, OUT_A, OUT_KV, OUT_Q = TT, 2 * TT, 3 * TT, 4 * TT
            OUT_LOG, OUT_G, OUT_U, OUT_D = 4 * TT + 1, 5 * TT + 1, 6 * TT + 1, 7 * TT + 1
            last_use = (OUT_WE, OUT_A, OUT_KV, OUT_Q, OUT_G, OUT_U, OUT_D)

            block = ctx.enter_context(nc.Block())

            def split_load(eng, n, src, r):
                wait(eng, pool_bl, n - 1)
                eng.dma_start(raw[r][:, :, :], src).then_inc(s_raw[r], 16)

            def split_hi(eng, r, sl, use, used_by, count):
                eng.wait_ge(s_raw[r], 16 * use + 16)
                wait(eng, used_by, count)
                eng.activation(bh[sl][:, :, :], raw[r][:, :, :], ACT.Copy).then_inc(act_bh, 1)

            def split_lo(eng, n, r, sl):
                eng.wait_ge(act_bh, n + 1)
                eng.tensor_tensor(bl[sl][:, :, :], raw[r][:, :, :], bh[sl][:, :, :].bitcast(F32), ALU.subtract)\
                   .then_inc(pool_bl, 1)

            @block.sync
            def _(eng):
                eng.dma_start(xt[:, :, :], rows(att_d)).then_inc(s_att, 16)
                eng.dma_start(xd[:, :, :], rows(den_d)).then_inc(s_att, 16)
                eng.dma_start(graw[:, :, :], rows(gate_wT)).then_inc(s_gw, 16)
                straight = [rows(we), rows(w_qkvaT)[:, :, 2 * D:3 * D], rows(w_qkvaT)[:, :, D:2 * D],
                            rows(w_qkvaT)[:, :, 0:D], rows(sguT)[:, :, 0:D], rows(sguT)[:, :, D:2 * D],
                            rows(sdownT), rows(w1T[0, :, :]), rows(w1T[1, :, :]), rows(w2T[0, :, :])]
                for n, src in enumerate(straight):
                    split_load(eng, n, src, n % 2)
                with eng.Fori(0, NEXP - 2) as e:
                    split_load(eng, e * 2 + NS + 3, rows(w1T[e + 2, :, :]), 0)
                    split_load(eng, e * 2 + NS + 4, rows(w2T[e + 1, :, :]), 1)
                split_load(eng, 2 * (NEXP - 2) + NS + 3, rows(w2T[NEXP - 1, :, :]), 0)
                eng.wait_ge(dve_acc, TT * NEXP)
                eng.dma_start(out.rearrange("(k p) n -> p k n", p=P), X[:, :, :]).then_inc(s_out, 16)
                eng.wait_ge(s_out, 16)

            @block.gpsimd
            def _(eng):
                eng.memset(before[:, :, :], 0.0).then_inc(tri, 1)
                eng.wait_ge(tri, 1)
                eng.affine_select(out=before[:, :, :], in_=before[:, :, :], compare_op=ALU.is_ge, fill=1.0, base=0,
                                  pattern=[[-1, NEXP], [1, NEXP]], channel_multiplier=0).then_inc(tri, 1)
                for n in range(NS + 3):
                    split_lo(eng, n, n % 2, slot(n))
                with eng.Fori(0, NEXP // 2 - 1) as i:
                    for u in range(2):
                        n = (i * 2 + u) * 2 + NS + 3
                        split_lo(eng, n, 0, W1[u])
                        split_lo(eng, n + 1, 1, W2[1 - u])
                split_lo(eng, 2 * (NEXP - 2) + NS + 3, 0, W2[1])

            @block.scalar
            def _(eng):
                def hi(n):
                    split_hi(eng, n % 2, slot(n), n // 2, pe_out, last_use[n - 4] if n >= 4 else 0)

                hi(0)
                for k in range(KT):
                    eng.wait_ge(dve_xt, k + 1)
                    eng.activation(AH[:, k, :], xt[:, k, :], ACT.Copy).then_inc(act_ah, 1)
                eng.wait_ge(s_gw, 16)
                eng.activation(gh[:, :, :], graw[:, :, :], ACT.Copy).then_inc(act_gh, 1)
                for n in (1, 2, 3):
                    hi(n)
                root_act(eng, 2)
                root_act(eng, 3)
                for k in range(KT):
                    eng.wait_ge(pe_tr, KT + k + 1)
                    eng.activation(AH[:, k, :], psum[:, k, :], ACT.Copy, scale=bcol[:, 2, k:k + 1]).then_inc(act_hi, 1)
                hi(4)
                for m in range(KT):
                    eng.wait_ge(pe_out, OUT_WE + m + 1)
                    eng.activation(gate[:, m, :], psum[:, m, :], ACT.Sigmoid).then_inc(act_sig, 1)
                for n in (5, 6, 7):
                    hi(n)
                root_act(eng, 4)
                for k in range(KT):
                    eng.wait_ge(pe_tr, 3 * KT + k + 1)
                    eng.activation(AH[:, k, :], psum[:, k, :], ACT.Copy).then_inc(act_hi, 1)
                eng.wait_ge(dve_logits, 1)
                eng.activation(pe[:, :, :], pr[:, :, :], ACT.Exp).then_inc(act_pe, 1)
                for m in range(KT):
                    eng.wait_ge(pe_out, OUT_LOG + m + 1)
                    eng.activation(gate[:, m, :], psum[:, m, :], ACT.Silu).then_inc(act_sg, 1)
                for m in range(KT):
                    eng.wait_ge(dve_gu, m + 1)
                    eng.activation(hh[0][:, m, :], y[:, m, :], ACT.Copy).then_inc(act_hs, 1)
                hi(8)
                hi(9)

                def silu(e, u):
                    wait(eng, dve_hl, KT * e)
                    wait(eng, pe_y, TT * (e - 1))
                    for m in range(KT):
                        eng.wait_ge(pe_h, KT * e + m + 1)
                        eng.activation(hf[:, m, :], psum[:, m, :], ACT.Silu).then_inc(act_silu, 1)
                    for m in range(KT):
                        eng.wait_ge(act_silu, KT * e + m + 1)
                        eng.activation(hh[u][:, m, :], hf[:, m, :], ACT.Copy).then_inc(act_hh, 1)

                silu(0, 0)

                def expert(e, u, w1=True):
                    if w1:
                        split_hi(eng, 0, W1[u], e + 5, pe_h, KT * (e + 1))
                    r = 1 if w1 else 0
                    if isinstance(e, int) and e == 0:
                        split_hi(eng, r, W2[1 - u], e + 5, pe_out, OUT_D)
                    else:
                        split_hi(eng, r, W2[1 - u], e + 5, pe_y, TT * e)
                    silu(e + 1, 1 - u)

                expert(0, 0)
                expert(1, 1)
                with eng.Fori(1, NEXP // 2 - 1) as i:
                    expert(i * 2, 0)
                    expert(i * 2 + 1, 1)
                expert(NEXP - 2, 0, w1=False)

            @block.tensor
            def _(eng):
                def weights(n):
                    eng.wait_ge(pool_bl, n + 1)
                    return bh[slot(n)], bl[slot(n)]

                eng.wait_ge(act_ah, KT)
                eng.wait_ge(dve_al, KT)
                h_, l_ = weights(WE)
                for t in range(TT):
                    product3(eng, psum[:, t, :], AH, AL, h_, l_, slice(t * P, (t + 1) * P)).then_inc(pe_out, 1)
                eng.wait_ge(dve_xs, TT)
                transpose_pe(eng)
                eng.wait_ge(act_hi, 2 * KT)
                eng.wait_ge(dve_lo, 2 * KT)
                for b, n in ((0, WA), (KT, WKV), (0, WQ)):
                    h_, l_ = weights(n)
                    for m in range(KT):
                        if n == WQ:
                            eng.wait_ge(act_sig, m + 1)
                        product3(eng, psum[:, b + m, :], h_, l_, AH, AL, slice(m * P, (m + 1) * P))\
                            .then_inc(pe_out, 1)
                eng.wait_ge(dve_qy, KT)
                for t in range(TT):
                    for k in range(KT):
                        ins = eng.transpose(psum[:, 4 + t, k * P:(k + 1) * P], y[:, k, t * P:(t + 1) * P], ident[:, :])
                    ins.then_inc(pe_tr, 1)
                eng.wait_ge(dve_xn, 3 * TT)
                transpose_pe(eng)
                eng.wait_ge(act_hi, 3 * KT)
                eng.wait_ge(dve_lo, 3 * KT)
                eng.wait_ge(act_gh, 1)
                eng.wait_ge(dve_gl, 1)
                for t in range(TT):
                    ins = product3(eng, psum[:, 4, t * NEXP:(t + 1) * NEXP], AH, AL, gh, gl, slice(t * P, (t + 1) * P))
                ins.then_inc(pe_out, 1)
                for b, n in ((0, SG), (KT, SU)):
                    h_, l_ = weights(n)
                    if n == SU:
                        eng.wait_ge(dve_logits, 1)
                    for m in range(KT):
                        product3(eng, psum[:, b + m, :], h_, l_, AH, AL, slice(m * P, (m + 1) * P))\
                            .then_inc(pe_out, 1)
                eng.wait_ge(act_hs, KT)
                eng.wait_ge(dve_hs, KT)
                h_, l_ = weights(SD)
                for t in range(TT):
                    product3(eng, psum[:, t, :], hh[0], hl[0], h_, l_, slice(t * P, (t + 1) * P)).then_inc(pe_out, 1)

                def first(e, u):
                    if isinstance(e, int) and e == 0:
                        eng.wait_ge(pool_bl, NS + 1)
                        eng.wait_ge(dve_x3, TT)
                    else:
                        eng.wait_ge(pool_bl, e * 2 + NS)
                    for m in range(KT):
                        wait(eng, act_silu, KT * (e - 1) + m + 1)
                        ins = product3(eng, psum[:, m, :], bh[W1[u]], bl[W1[u]], AH, AL, slice(m * P, (m + 1) * P))
                        ins.then_inc(pe_h, 1)

                def second(e, u, last=False):
                    eng.wait_ge(pool_bl, e * 2 + NS + 3 - (1 if last else 0))
                    eng.wait_ge(dve_hl, KT * (e + 1))
                    eng.wait_ge(act_hh, KT * (e + 1))
                    for t in range(TT):
                        wait(eng, dve_acc, TT * (e - 1) + t + 1)
                        ins = product3(eng, psum[:, 4 + t, :], hh[u], hl[u], bh[W2[u]], bl[W2[u]],
                                       slice(t * P, (t + 1) * P))
                        ins.then_inc(pe_y, 1)

                first(0, 0)

                def expert(e, u, last=False):
                    if not last:
                        first(e + 1, 1 - u)
                    second(e, u, last)

                expert(0, 0)
                expert(1, 1)
                with eng.Fori(1, NEXP // 2 - 1) as i:
                    expert(i * 2, 0)
                    expert(i * 2 + 1, 1)
                expert(NEXP - 2, 0)
                expert(NEXP - 1, 1, last=True)

            @block.vector
            def _(eng):
                for t in range(TT):
                    ins = eng.tensor_tensor(X[:, t, :], X[:, t, :], brow[:, 1, :], ALU.add)
                link(eng, ins)
                eng.wait_ge(s_att, 32)
                for k in range(KT):
                    eng.reciprocal(xd[:, k, :], xd[:, k, :]).then_inc(dve_xd, 1)
                    eng.wait_ge(dve_xd, k + 1)
                    eng.tensor_tensor(xt[:, k, :], xt[:, k, :], xd[:, k, :], ALU.mult).then_inc(dve_xt, 1)
                for k in range(KT):
                    eng.wait_ge(act_ah, k + 1)
                    eng.tensor_tensor(AL[:, k, :], xt[:, k, :], AH[:, k, :].bitcast(F32), ALU.subtract)\
                       .then_inc(dve_al, 1)
                eng.wait_ge(act_gh, 1)
                eng.tensor_tensor(gl[:, :, :], graw[:, :, :], gh[:, :, :].bitcast(F32), ALU.subtract)\
                   .then_inc(dve_gl, 1)
                for t in range(TT):
                    eng.wait_ge(pe_out, t + 1)
                    ins = eng.tensor_tensor(X[:, t, :], X[:, t, :], psum[:, t, :], ALU.add)
                link(eng, ins)
                layer_norm_dve(eng)
                eng.wait_ge(dve_xn, 2 * TT)
                for t in range(TT):
                    ins = eng.tensor_tensor_reduce(y[:, t, :], XN[:, t, :], XN[:, t, :], 1.0, 0.0, ALU.mult, ALU.add,
                                                   ss[:, t:t + 1])
                link(eng, ins)
                eng.tensor_scalar(ve[:, :], ss[:, :], NORM_EPS * NORM_EPS, None, ALU.max).then_inc(dve_ve, 1)
                inverse_root_dve(eng)
                for t in range(TT):
                    eng.tensor_scalar(XN[:, t, :], XN[:, t, :], rs[:, t:t + 1], float(D) ** 0.5, ALU.mult, ALU.mult)\
                       .then_inc(dve_xs, 1)
                for k in range(KT):
                    eng.wait_ge(act_hi, KT + k + 1)
                    eng.scalar_tensor_tensor(out=AL[:, k, :], in0=psum[:, k, :], scalar=bcol[:, 2, k:k + 1],
                                             in1=AH[:, k, :].bitcast(F32), op0=ALU.mult, op1=ALU.subtract)\
                       .then_inc(dve_lo, 1)
                for m in range(KT):
                    eng.wait_ge(act_sig, m + 1)
                    eng.wait_ge(pe_out, OUT_A + m + 1)
                    eng.tensor_tensor_scan(y[:, m, :], gate[:, m, :], psum[:, KT + m, :], 0.0, ALU.mult, ALU.add)\
                       .then_inc(dve_y, 1)
                for m in range(KT):
                    eng.wait_ge(dve_y, m + 1)
                    eng.wait_ge(pe_out, OUT_KV + m + 1)
                    eng.tensor_tensor(y[:, m, :], y[:, m, :], psum[:, m, :], ALU.mult).then_inc(dve_qy, 1)
                for t in range(TT):
                    eng.wait_ge(pe_tr, 2 * KT + t + 1)
                    ins = eng.tensor_tensor(X[:, t, :], X[:, t, :], psum[:, 4 + t, :], ALU.add)
                link(eng, ins)
                layer_norm_dve(eng)
                for k in range(KT):
                    eng.wait_ge(act_hi, 2 * KT + k + 1)
                    eng.tensor_tensor(AL[:, k, :], psum[:, k, :], AH[:, k, :].bitcast(F32), ALU.subtract)\
                       .then_inc(dve_lo, 1)

                def over_experts(ap):
                    return ap.unsqueeze(2).to_broadcast([P, TT, NEXP])

                logits = psum[:, 4, 0:TT * NEXP].rearrange("p (t e) -> p t e", e=NEXP)
                eng.wait_ge(pe_out, OUT_LOG)
                link(eng, eng.tensor_reduce(r1[:, :], logits, AX.X, ALU.max))
                eng.tensor_tensor(pr[:, :, :], logits, over_experts(r1[:, :]), ALU.subtract).then_inc(dve_logits, 1)
                for m in range(KT):
                    eng.wait_ge(act_sg, m + 1)
                    eng.wait_ge(pe_out, OUT_G + m + 1)
                    eng.tensor_tensor(y[:, m, :], gate[:, m, :], psum[:, KT + m, :], ALU.mult).then_inc(dve_gu, 1)
                for m in range(KT):
                    eng.wait_ge(act_hs, m + 1)
                    eng.tensor_tensor(hl[0][:, m, :], y[:, m, :], hh[0][:, m, :].bitcast(F32), ALU.subtract)\
                       .then_inc(dve_hs, 1)
                eng.wait_ge(act_pe, 1)
                link(eng, eng.tensor_reduce(r1[:, :], pe[:, :, :], AX.X, ALU.add))
                link(eng, eng.reciprocal(t0[:, :], r1[:, :]))
                link(eng, eng.tensor_tensor(pr[:, :, :], pe[:, :, :], over_experts(t0[:, :]), ALU.mult))
                mine = pr[:, :, :].unsqueeze(3).to_broadcast([P, TT, NEXP, NEXP])
                other = pr[:, :, :].unsqueeze(2).to_broadcast([P, TT, NEXP, NEXP])
                link(eng, eng.tensor_tensor(cmp_[:, :, :, :], other, mine, ALU.is_gt))
                link(eng, eng.tensor_tensor(eq_[:, :, :, :], other, mine, ALU.is_equal))
                eng.wait_ge(tri, 2)
                link(eng, eng.tensor_tensor(eq_[:, :, :, :], eq_[:, :, :, :],
                                            before[:, :, :].unsqueeze(1).to_broadcast([P, TT, NEXP, NEXP]), ALU.mult))
                link(eng, eng.tensor_tensor(cmp_[:, :, :, :], cmp_[:, :, :, :], eq_[:, :, :, :], ALU.add))
                link(eng, eng.tensor_reduce(rank[:, :, :], cmp_[:, :, :, :], AX.X, ALU.add))
                link(eng, eng.tensor_scalar(rank[:, :, :], rank[:, :, :], float(TOPK), None, ALU.is_lt))
                link(eng, eng.tensor_tensor(wt[:, :, :], pr[:, :, :], rank[:, :, :], ALU.mult))
                link(eng, eng.tensor_reduce(r1[:, :], wt[:, :, :], AX.X, ALU.add))
                link(eng, eng.reciprocal(t0[:, :], r1[:, :]))
                link(eng, eng.tensor_tensor(wt[:, :, :], wt[:, :, :], over_experts(t0[:, :]), ALU.mult))
                for t in range(TT):
                    eng.wait_ge(pe_out, OUT_U + t + 1)
                    eng.tensor_tensor(X[:, t, :], X[:, t, :], psum[:, t, :], ALU.add).then_inc(dve_x3, 1)

                def split(e, u):
                    for m in range(KT):
                        eng.wait_ge(act_hh, KT * e + m + 1)
                        eng.tensor_tensor(hl[u][:, m, :], hf[:, m, :], hh[u][:, m, :].bitcast(F32), ALU.subtract)\
                           .then_inc(dve_hl, 1)

                def expert(e, u, last=False):
                    if not last:
                        split(e + 1, 1 - u)
                    for t in range(TT):
                        eng.wait_ge(pe_y, TT * e + t + 1)
                        if isinstance(e, int) and e == 0:
                            eng.wait_ge(dve_x3, t + 1)
                        else:
                            eng.wait_ge(dve_acc, TT * (e - 1) + t + 1)
                        eng.scalar_tensor_tensor(out=X[:, t, :], in0=psum[:, 4 + t, :],
                                                 scalar=wt[:, t, :][:, bass.ds(e, 1)], in1=X[:, t, :],
                                                 op0=ALU.mult, op1=ALU.add).then_inc(dve_acc, 1)

                split(0, 0)
                expert(0, 0)
                expert(1, 1)
                with eng.Fori(1, NEXP // 2 - 1) as i:
                    expert(i * 2, 0)
                    expert(i * 2 + 1, 1)
                expert(NEXP - 2, 0)
                expert(NEXP - 1, 1, last=True)


def kernel(**inputs):
    import numpy as np
    import concourse.bacc as bacc
    from concourse.bass_utils import run_bass_kernel_spmd

    def columns(v):
        return np.ascontiguousarray(np.asarray(v).reshape(KT, P).T)

    def transposed(a):
        return np.ascontiguousarray(np.swapaxes(np.asarray(a), -1, -2))

    laid_out = {
        "x": np.asarray(inputs["x"])[0],
        "ctxT": transposed(inputs["ctx_1024"])[0],
        "wq": inputs["L0_xattn_Wq"], "bq": columns(inputs["L0_xattn_bq"]),
        "wk": inputs["L0_xattn_Wk"], "bk": columns(inputs["L0_xattn_bk"]),
        "wv": inputs["L0_xattn_Wv"], "bv": np.asarray(inputs["L0_xattn_bv"]).reshape(1, D),
        "we": inputs["L0_xattn_We"], "be": np.asarray(inputs["L0_xattn_be"]).reshape(1, D),
        "w_qkvaT": transposed(inputs["L0_attn_W_qkva"]), "gamma": columns(inputs["L0_attn_gamma"]),
        "gate_wT": transposed(inputs["L0_ffn_gate_w"]),
        "w1T": transposed(inputs["L0_ffn_w1"]), "w2T": transposed(inputs["L0_ffn_w2"]),
        "sguT": transposed(inputs["L0_ffn_shared_gu"]), "sdownT": transposed(inputs["L0_ffn_shared_down"]),
    }
    nc = bacc.Bacc("TRN2", target_bir_lowering=False, num_devices=1)
    arrays, args = {}, []
    for name, a in laid_out.items():
        a = np.ascontiguousarray(a)
        arrays[name + "_dram"] = a
        args.append(nc.dram_tensor(name + "_dram", a.shape, mybir.dt.from_np(a.dtype), kind="ExternalInput").ap())
    args.append(nc.dram_tensor("out_dram", (T, D), F32, kind="ExternalOutput").ap())
    perceiver_program(nc, *args)
    r = run_bass_kernel_spmd(nc, [arrays], core_ids=[0])
    return np.asarray(r.results[0]["out_dram"]).reshape(1, T, D)
```

```python
from contextlib import ExitStack

import concourse.bass as bass
from concourse import mybir

F32 = mybir.dt.float32
F32R = mybir.dt.float32r
ALU = mybir.AluOpType
ACT = mybir.ActivationFunctionType
AX = mybir.AxisListType

P = 128
D = 512
KT = D // P
T = 512
TT = T // P
S = 8192
H = 16
E = D // H
HT = P // E
CH = 512
NCH = S // CH
KEYT = S // P
NG = KEYT // 4
QUARTERS = 4
QK = S // QUARTERS
NEXP = 16
TOPK = 4
LN_EPS = 1e-5
NORM_EPS = 1e-12
SCALE = float(E) ** -0.5

PASS1_GROUPS = 14


PASS1 = [("max", k // TT, k % TT) for k in range(NCH * TT)]
RING = (5, 6, 7)
ITEMS = len(PASS1) + 2
LATE_CHUNKS = (0, 1, NCH - 2, NCH - 1)
EARLY = (NCH - len(LATE_CHUNKS)) * TT
LATE = [(EARLY + n, ("max", LATE_CHUNKS[n // TT], n % TT)) for n in range(TT * len(LATE_CHUNKS))]
SUM = 2 * len(PASS1) // PASS1_GROUPS

SROWS = 3 * E + 2
PAIRS = KEYT // 2
SLOTS = 6
POOL_PAIRS = KEYT // 3
POOL_ADDS = POOL_PAIRS - 1


def slot_of(u, p):
    return (p + SLOTS // 2 * u) % SLOTS


def slot_before(u, p):
    for back in range(1, 2 * SLOTS):
        q = p - back
        if q >= 0 and slot_of(u, q) == slot_of(u, p) or q < 0 and slot_of(1 - u, q + PAIRS) == slot_of(u, p):
            return back, q % PAIRS


def pool_adds(p):
    return max([1] + [t // 3 for t in (2 * p, 2 * p + 1) if t % 3])


def number(n):
    return n + 1 if n >= SUM else n


def schedule(first, last):
    out = []
    n = len(PASS1)
    for g in range(NG):
        mine = [] if last else [("item", number(k)) + PASS1[k] for k in
                                range(min(n, g * n // PASS1_GROUPS), min(n, (g + 1) * n // PASS1_GROUPS))]
        cuts = [mine[0:1], mine[1:2], mine[2:3], mine[3:]]
        if g == 1 and not first:
            cuts[3] = cuts[3] + [("item", SUM, "sum", 0, 0)]
        if g == NG - 1 and not last:
            cuts[0] = cuts[0] + [("item", ITEMS - 1, "neg", 0, 0)]
        pv = [("pv", (g - 1) % NG, b) for b in range(2)] if g > 0 or not first else []
        out += [("st", g, 0)] + cuts[0] + [("st", g, 1)] + cuts[1] + cuts[2] + pv + cuts[3]
    return out


def ring_at(h, k):
    banks, bank = len(RING), k % len(RING)
    if isinstance(h, int) and h == H - 1:
        k = 0
    left_out = [number(n) for n in range(EARLY)] + [SUM, ITEMS + SUM]
    if isinstance(h, int) and h < 1:
        left_out = [n for n in left_out if n < (h + 1) * ITEMS + k]
    return ((h + 1) * ITEMS + k - len(left_out),
            (h + 1) * (ITEMS // banks) + k // banks - len([n for n in left_out if n % banks == bank]), bank)


def wait(eng, sem, value):
    if isinstance(value, int) and value <= 0:
        return
    eng.wait_ge(sem, value)


def perceiver_program(nc, x, ctxT, wq, bq, wk, bk, wv, bv, we, be, w_qkvaT, gamma, gate_wT, w1T, w2T,
                      sguT, sdownT, out):
    def rows(ap):
        return ap.rearrange("(k p) n -> p k n", p=P)

    kh_d = nc.dram_tensor("kh_scratch", (D, S), F32, kind="Internal").ap()
    kl_d = nc.dram_tensor("kl_scratch", (D, S), F32, kind="Internal").ap()
    qh_d = nc.dram_tensor("qh_scratch", (D, T), F32, kind="Internal").ap()
    ql_d = nc.dram_tensor("ql_scratch", (D, T), F32, kind="Internal").ap()
    v_d = nc.dram_tensor("v_scratch", (H, P, KEYT * E), F32, kind="Internal").ap()
    att_d = nc.dram_tensor("att_scratch", (D, T), F32, kind="Internal").ap()
    den_d = nc.dram_tensor("den_scratch", (D, T), F32, kind="Internal").ap()

    with ExitStack() as whole:
        def alloc(ctx):
            return (lambda name, shape, dt=F32: ctx.enter_context(nc.sbuf_tensor(name, shape, dt)))

        def sem(name):
            return whole.enter_context(nc.semaphore(name))

        sb = alloc(whole)
        psum = whole.enter_context(nc.psum_tensor("psum", [P, 8, 512], F32))

        X = sb("X", [P, TT, D])
        XN = sb("XN", [P, TT, D])
        AH = sb("AH", [P, KT, T], F32R)
        AL = sb("AL", [P, KT, T], F32R)
        ident = sb("ident", [P, P])
        stats = sb("stats", [P, TT, 6])
        mv = sb("mv", [P, TT, 2])
        ve = sb("ve", [P, TT])
        sd = sb("sd", [P, TT])
        rs = sb("rs", [P, TT])
        t0 = sb("t0", [P, TT])
        warm = sb("warm", [P, 8])
        bcol = sb("bcol", [P, 3, KT])
        mx = sb("mx", [P, TT, NCH])
        brow = sb("brow", [P, 2, D])

        s_ident = sem("s_ident")
        s_x = sem("s_x")
        s_kv_bias = sem("s_kv_bias")
        s_small = sem("s_small")
        dve_step = sem("dve_step")
        dve_ve = sem("dve_ve")
        act_sqrt = sem("act_sqrt")
        pe_tr = sem("pe_tr")
        act_hi = sem("act_hi")
        dve_lo = sem("dve_lo")
        dve_xn = sem("dve_xn")
        pe_out = sem("pe_out")
        dve_added = sem("dve_added")

        steps = [0]

        def link(eng, ins):
            steps[0] += 1
            ins.then_inc(dve_step, 1)
            eng.wait_ge(dve_step, steps[0])

        roots = [0]

        def inverse_root_dve(eng):
            roots[0] += 1
            eng.wait_ge(act_sqrt, roots[0])
            link(eng, eng.reciprocal(t0[:, :], sd[:, :]))
            link(eng, eng.scalar_tensor_tensor(out=t0[:, :], in0=t0[:, :], scalar=0.5, in1=ve[:, :],
                                               op0=ALU.mult, op1=ALU.mult))
            link(eng, eng.scalar_tensor_tensor(out=t0[:, :], in0=sd[:, :], scalar=0.5, in1=t0[:, :],
                                               op0=ALU.mult, op1=ALU.add))
            link(eng, eng.reciprocal(rs[:, :], t0[:, :]))

        adds = [0]

        def row_moments_dve(eng, add=None):
            for t in range(TT):
                if add is not None:
                    adds[0] += 1
                    add(t).then_inc(dve_added, 1)
                    eng.wait_ge(dve_added, adds[0])
                ins = eng.bn_stats(stats[:, t, :], X[:, t, :])
            link(eng, ins)
            for t in range(TT):
                ins = eng.bn_aggr(mv[:, t, :], stats[:, t, :])
            link(eng, ins)

        def layer_norm_dve(eng, add=None):
            row_moments_dve(eng, add)
            eng.tensor_scalar(ve[:, :], mv[:, :, 1], LN_EPS, None, ALU.add).then_inc(dve_ve, 1)
            inverse_root_dve(eng)
            for t in range(TT):
                eng.tensor_scalar(XN[:, t, :], X[:, t, :], mv[:, t, 0:1], rs[:, t:t + 1],
                                  ALU.subtract, ALU.mult).then_inc(dve_xn, 1)

        preloads = [0]

        def preload(eng, func):
            eng.activation(warm[:, preloads[0]:preloads[0] + 1], ident[:, 0:1], func)
            preloads[0] += 1

        def root_act(eng, n):
            preload(eng, ACT.Sqrt)
            eng.wait_ge(dve_ve, n)
            eng.activation(sd[:, :], ve[:, :], ACT.Sqrt).then_inc(act_sqrt, 1)

        def transpose_pe(eng, rows_before):
            for t in range(TT):
                eng.wait_ge(dve_xn, rows_before + t + 1)
                for k in range(KT):
                    ins = eng.transpose(psum[:, k, t * P:(t + 1) * P], XN[:, t, k * P:(k + 1) * P], ident[:, :])
                    if t == TT - 1:
                        ins.then_inc(pe_tr, 1)

        def product3(eng, bank_ap, lh, ll, rh, rl, m=None, ready=None):
            n = 0
            for k in range(KT):
                if ready is not None:
                    eng.wait_ge(ready[0], ready[2] + k + 1)
                    eng.wait_ge(ready[1], ready[2] + k + 1)
                for left, right in ((lh, rh), (lh, rl), (ll, rh)):
                    ins = eng.matmul(bank_ap, left[:, k, m], right[:, k, :], start=(n == 0), stop=(n == 3 * KT - 1))
                    n += 1
            return ins

        with ExitStack() as ctx:
            sb1 = alloc(ctx)
            wraw = sb1("wraw", [P, 3, KT, D])
            wh = sb1("wh", [P, 3, KT, D], F32R)
            wl = sb1("wl", [P, 3, KT, D], F32R)
            craw = sb1("craw", [P, 2, KT, CH])
            chi = sb1("chi", [P, 2, KT, CH], F32R)
            clo = sb1("clo", [P, 2, KT, CH], F32R)
            q32 = XN
            khi = sb1("khi", [P, KT, CH], F32R)
            klo = sb1("klo", [P, KT, CH], F32R)
            vsb = sb1("vsb", [P, H, 4, E])
            qfirst = sb1("qfirst", [3 * E, T], F32R)
            kfirst = sb1("kfirst", [3 * E, 2, CH], F32R)

            FIRST = 7
            VBANK = (4, 5, 6, 4)
            WQ, WK, WV = range(3)
            ORDER = (WV, WQ)
            s_w = [sem(f"s_w{n}") for n in range(3)]
            s_begin = [sem(f"s_begin{k}") for k in range(KT)]
            begin_hi = sem("begin_hi")
            begin_wl = sem("begin_wl")
            begin_cl = sem("begin_cl")
            act_wh = sem("act_wh")
            pool_wl = sem("pool_wl")
            pe_q = sem("pe_q")
            dve_q = sem("dve_q")
            dve_ql = sem("dve_ql")
            act_qh = sem("act_qh")
            s_qst = sem("s_qst")
            s_c = [sem(f"s_c{n}") for n in range(2)]
            act_ch = sem("act_ch")
            dve_cl = sem("dve_cl")
            pe_k = sem("pe_k")
            pe_v = sem("pe_v")
            act_kh = sem("act_kh")
            dve_kl = sem("dve_kl")
            dve_v = sem("dve_v")
            s_qf = sem("s_qf")
            s_kf = [sem(f"s_kf{n}") for n in range(2)]
            first_ready = sem("first_ready")
            first_taken = sem("first_taken")
            s_we = sem("s_we")
            we_hi = sem("we_hi")
            we_lo = sem("we_lo")
            s_kvst = sem("s_kvst")

            block = ctx.enter_context(nc.Block())

            @block.sync
            def _(eng):
                def load_w(n, w):
                    eng.dma_start(wraw[:, n, :, :], rows(w)).then_inc(s_w[n], 16)

                for k in range(KT):
                    eng.dma_start(wraw[:, WK, k, :], wk[k * P:(k + 1) * P, :]).then_inc(s_begin[k], 16)
                    eng.dma_start(craw[:, 0, k, :], ctxT[k * P:(k + 1) * P, 0:CH]).then_inc(s_begin[k], 16)
                eng.dma_start(bcol[:, 1, :], bk).then_inc(s_kv_bias, 16)
                eng.dma_start(brow[:, 0, :], bv.to_broadcast([P, D])).then_inc(s_kv_bias, 16)
                load_w(WV, wv)
                eng.dma_start(craw[:, 1, :, :], rows(ctxT)[:, :, CH:2 * CH]).then_inc(s_c[1], 16)
                eng.dma_start(X[:, :, :], x.rearrange("(k p) n -> p k n", p=P)).then_inc(s_x, 16)
                load_w(WQ, wq)
                eng.dma_start(bcol[:, 0, :], bq).then_inc(s_small, 16)
                eng.dma_start(bcol[:, 2, :], gamma).then_inc(s_small, 16)
                eng.dma_start(brow[:, 1, :], be.to_broadcast([P, D])).then_inc(s_small, 16)
                def load_chunks(i, keys):
                    for u in range(2):
                        if u == 0 and not keys:
                            eng.wait_ge(begin_cl, KT)
                        else:
                            eng.wait_ge(dve_cl, i * 2 + u - 2)
                        eng.dma_start(craw[:, u, :, :], rows(ctxT)[:, :, bass.ds((i * 2 + u) * CH, CH)])\
                           .then_inc(s_c[u], 16)
                        if keys:
                            eng.wait_ge(s_kvst, 48 * (i * 2 + u - 1))
                            for part, src in enumerate((kh_d, kh_d, kl_d)):
                                eng.dma_start(kfirst[part * E:(part + 1) * E, u, :].bitcast(F32),
                                              src[0:E, bass.ds((i * 2 + u - 2) * CH, CH)]).then_inc(s_kf[u], 16)

                load_chunks(1, keys=False)
                with eng.Fori(2, NCH // 2) as i:
                    load_chunks(i, keys=True)

            @block.gpsimd
            def _(eng):
                eng.memset(ident[:, :], 0.0).then_inc(s_ident, 1)
                eng.wait_ge(s_ident, 1)
                eng.affine_select(out=ident[:, :], in_=ident[:, :], compare_op=ALU.not_equal, fill=1.0, base=0,
                                  pattern=[[-1, P]], channel_multiplier=1).then_inc(s_ident, 1)
                for k in range(KT):
                    eng.wait_ge(begin_hi, k + 1)
                    eng.tensor_tensor(wl[:, WK, k, :], wraw[:, WK, k, :], wh[:, WK, k, :].bitcast(F32), ALU.subtract)\
                       .then_inc(begin_wl, 1)
                for n, w in enumerate(ORDER):
                    eng.wait_ge(act_wh, n + 1)
                    eng.tensor_tensor(wl[:, w, :, :], wraw[:, w, :, :], wh[:, w, :, :].bitcast(F32), ALU.subtract)\
                       .then_inc(pool_wl, 1)
                eng.wait_ge(s_qst, 32)
                for part, src in enumerate((qh_d, ql_d, qh_d)):
                    eng.dma_start(qfirst[part * E:(part + 1) * E, :].bitcast(F32), src[0:E, :]).then_inc(s_qf, 16)
                eng.wait_ge(pool_wl, 2)
                eng.dma_start(wraw[:, WQ, :, :], rows(we)).then_inc(s_we, 16)
                eng.wait_ge(we_hi, 1)
                eng.tensor_tensor(AL[:, :, :], wraw[:, WQ, :, :], AH[:, :, :].bitcast(F32), ALU.subtract)\
                   .then_inc(we_lo, 1)

            @block.scalar
            def _(eng):
                def high_w(w):
                    eng.wait_ge(s_w[w], 16)
                    eng.activation(wh[:, w, :, :], wraw[:, w, :, :], ACT.Copy).then_inc(act_wh, 1)

                def split(i, u):
                    c = i * 2 + u
                    eng.wait_ge(s_c[u], 16 * (i + u))
                    wait(eng, pe_v, 4 * (c - 1))
                    eng.activation(chi[:, u, :, :], craw[:, u, :, :], ACT.Copy).then_inc(act_ch, 1)

                def chunk(i, u, last=False, queries=False):
                    c = i * 2 + u
                    if not last:
                        split(i + u, 1 - u)
                    wait(eng, s_kvst, 48 * c)
                    for m in range(KT):
                        eng.wait_ge(pe_k, 4 * c + m + 1)
                        eng.activation(khi[:, m, :], psum[:, m, :], ACT.Identity, bias=bcol[:, 1, m:m + 1])\
                           .then_inc(act_kh, 1)
                    if queries:
                        for k in range(KT):
                            eng.wait_ge(pe_tr, k + 1)
                            eng.activation(AH[:, k, :], psum[:, k, :], ACT.Copy).then_inc(act_hi, 1)
                    cols = bass.ds(c * CH, CH)
                    eng.wait_ge(act_kh, 4 * c + 4)
                    eng.dma_start(rows(kh_d)[:, :, cols], khi[:, :, :].bitcast(F32)).then_inc(s_kvst, 16)
                    eng.wait_ge(dve_kl, 4 * c + 4)
                    eng.dma_start(rows(kl_d)[:, :, cols], klo[:, :, :].bitcast(F32)).then_inc(s_kvst, 16)
                    eng.wait_ge(dve_v, 4 * c + 4)
                    eng.dma_start(v_d.rearrange("h p n -> p h n")[:, :, bass.ds(c * 4 * E, 4 * E)],
                                  vsb[:, :, :, :].rearrange("p h t e -> p h (t e)")).then_inc(s_kvst, 16)

                for k in range(KT):
                    eng.wait_ge(s_begin[k], 32)
                    eng.activation(wh[:, WK, k, :], wraw[:, WK, k, :], ACT.Copy)
                    eng.activation(chi[:, 0, k, :], craw[:, 0, k, :], ACT.Copy).then_inc(begin_hi, 1)
                high_w(WV)
                eng.wait_ge(s_kv_bias, 16 * 2)
                chunk(0, 0)
                eng.wait_ge(s_ident, 2)
                root_act(eng, 1)
                high_w(WQ)
                chunk(0, 1, queries=True)
                for m in range(KT):
                    eng.wait_ge(pe_q, KT)
                    eng.wait_ge(dve_q, m + 1)
                    eng.activation(AH[:, m, :], q32[:, m, :], ACT.Copy).then_inc(act_qh, 1)
                eng.wait_ge(act_qh, KT)
                eng.dma_start(rows(qh_d), AH[:, :, :].bitcast(F32)).then_inc(s_qst, 16)
                eng.wait_ge(dve_ql, KT)
                eng.dma_start(rows(ql_d), AL[:, :, :].bitcast(F32)).then_inc(s_qst, 16)
                with eng.Fori(1, NCH // 2 - 1) as i:
                    chunk(i, 0)
                    chunk(i, 1)
                eng.wait_ge(s_we, 16)
                eng.wait_ge(s_qst, 32)
                eng.activation(AH[:, :, :], wraw[:, WQ, :, :], ACT.Copy).then_inc(we_hi, 1)
                chunk(NCH // 2 - 1, 0)
                chunk(NCH // 2 - 1, 1, last=True)
                eng.wait_ge(s_kvst, 48 * NCH)

            @block.tensor
            def _(eng):
                def keys(c, u, ready=None):
                    for m in range(KT):
                        wait(eng, dve_kl, 4 * (c - 1) + m + 1)
                        product3(eng, psum[:, m, :], wh[:, WK, :, :], wl[:, WK, :, :], chi[:, u, :, :], clo[:, u, :, :],
                                 slice(m * P, (m + 1) * P), ready=ready if m == 0 else None).then_inc(pe_k, 1)

                def values(i, u, first=True):
                    c = i * 2 + u
                    for t in range(4):
                        if first:
                            if t == 0:
                                eng.wait_ge(s_kf[u], 48 * (i - 1))
                            wait(eng, first_taken, 4 * (c - 4) + t)
                            eng.matmul(psum[:, FIRST, :], qfirst[:, t * P:(t + 1) * P], kfirst[:, u, :],
                                       start=True, stop=True).then_inc(first_ready, 1)
                        wait(eng, dve_v, 4 * c + 1 if t == 3 else 4 * (c - 1) + (t + 1 if t else 4))
                        product3(eng, psum[:, VBANK[t], :], chi[:, u, :, :], clo[:, u, :, :], wh[:, WV, :, :],
                                 wl[:, WV, :, :], slice(t * P, (t + 1) * P)).then_inc(pe_v, 1)

                def chunk(i, u, first=True):
                    c = i * 2 + u
                    eng.wait_ge(act_ch, c)
                    eng.wait_ge(dve_cl, c)
                    keys(c, u)
                    values(i, u, first)

                keys(0, 0, ready=(begin_wl, begin_cl, 0))
                eng.wait_ge(act_wh, 1)
                eng.wait_ge(pool_wl, 1)
                values(0, 0, first=False)
                eng.wait_ge(act_ch, 1)
                eng.wait_ge(dve_cl, 1)
                keys(1, 1)
                eng.wait_ge(s_ident, 2)
                eng.wait_ge(act_kh, 2 * KT)
                eng.wait_ge(dve_kl, 2 * KT)
                transpose_pe(eng, 0)
                values(0, 1, first=False)
                eng.wait_ge(act_hi, KT)
                eng.wait_ge(dve_lo, KT)
                eng.wait_ge(act_wh, 2)
                eng.wait_ge(pool_wl, 2)
                for m in range(KT):
                    product3(eng, psum[:, m, :], wh[:, WQ, :, :], wl[:, WQ, :, :], AH, AL,
                             slice(m * P, (m + 1) * P)).then_inc(pe_q, 1)
                eng.wait_ge(dve_q, KT)
                chunk(1, 0, first=False)
                chunk(1, 1, first=False)
                eng.wait_ge(s_qf, 48)
                chunk(2, 0)
                chunk(2, 1)
                with eng.Fori(3, NCH // 2) as i:
                    chunk(i, 0)
                    chunk(i, 1)

            @block.vector
            def _(eng):
                def split(c, u):
                    eng.wait_ge(act_ch, c)
                    eng.tensor_tensor(clo[:, u, :, :], craw[:, u, :, :], chi[:, u, :, :].bitcast(F32), ALU.subtract)\
                       .then_inc(dve_cl, 1)

                def chunk(i, u, last=False, queries=False, first=True):
                    c = i * 2 + u
                    if not last:
                        split(c + 1, 1 - u)
                    for m in range(KT):
                        eng.wait_ge(act_kh, 4 * c + m + 1)
                        eng.scalar_tensor_tensor(out=klo[:, m, :], in0=psum[:, m, :], scalar=bcol[:, 1, m:m + 1],
                                                 in1=khi[:, m, :].bitcast(F32), op0=ALU.add, op1=ALU.subtract)\
                           .then_inc(dve_kl, 1)
                    if queries:
                        for k in range(KT):
                            eng.wait_ge(act_hi, k + 1)
                            eng.tensor_tensor(AL[:, k, :], psum[:, k, :], AH[:, k, :].bitcast(F32), ALU.subtract)\
                               .then_inc(dve_lo, 1)
                    wait(eng, s_kvst, 48 * c)
                    for t in range(4):
                        if first:
                            eng.wait_ge(first_ready, 4 * (c - 4) + t + 1)
                            eng.tensor_reduce(mx[:, t, :][:, bass.ds(c - 2, 1)], psum[:, FIRST, :], AX.X, ALU.max)\
                               .then_inc(first_taken, 1)
                        eng.wait_ge(pe_v, 4 * c + t + 1)
                        eng.tensor_tensor(vsb[:, :, t, :], psum[:, VBANK[t], :].rearrange("p (h e) -> p h e", e=E),
                                          brow[:, 0, :].rearrange("p (h e) -> p h e", e=E), ALU.add)\
                           .then_inc(dve_v, 1)

                for k in range(KT):
                    eng.wait_ge(begin_hi, k + 1)
                    eng.tensor_tensor(clo[:, 0, k, :], craw[:, 0, k, :], chi[:, 0, k, :].bitcast(F32), ALU.subtract)\
                       .then_inc(begin_cl, 1)
                eng.wait_ge(s_kv_bias, 16 * 2)
                chunk(0, 0, first=False)
                eng.wait_ge(s_x, 16)
                layer_norm_dve(eng)
                chunk(0, 1, queries=True, first=False)
                eng.wait_ge(s_small, 16 * 3)
                for m in range(KT):
                    eng.wait_ge(pe_q, m + 1)
                    eng.tensor_scalar(q32[:, m, :], psum[:, m, :], bcol[:, 0, m:m + 1], SCALE,
                                      ALU.add, ALU.mult).then_inc(dve_q, 1)
                for m in range(KT):
                    eng.wait_ge(act_qh, m + 1)
                    eng.tensor_tensor(AL[:, m, :], q32[:, m, :], AH[:, m, :].bitcast(F32), ALU.subtract)\
                       .then_inc(dve_ql, 1)
                chunk(1, 0, first=False)
                chunk(1, 1, first=False)
                with eng.Fori(2, NCH // 2 - 1) as i:
                    chunk(i, 0)
                    chunk(i, 1)
                chunk(NCH // 2 - 1, 0)
                chunk(NCH // 2 - 1, 1, last=True)

        with ExitStack() as ctx:
            sb2 = alloc(ctx)
            ks = [sb2(f"ks{n}", [P, S], F32R) for n in range(2)]
            qmax = [sb2(f"qmax{n}", [P, T], F32R) for n in range(2)]
            qexp = [sb2(f"qexp{n}", [P, T], F32R) for n in range(2)]
            vh = [sb2(f"vh{n}", [P, KEYT, E]) for n in range(2)]
            prob = sb2("prob", [P, 2 * SLOTS, T])
            pool_sum = [sb2(f"pool_sum{n}", [P, 2, T]) for n in range(2)]
            ones = sb2("ones", [P, E])
            sel = sb2("sel", [P, 2 * E])
            m4 = sb2("m4", [P, TT])
            nm = sb2("nm", [P, TT, E], F32R)
            xd = sb2("xd", [P, KT, T])
            osb = sb2("osb", [P, T])
            att = [sb2(f"att{n}", [2 * E, T]) for n in range(2)]

            const_c = sem("const_c")
            s_kq = [[sem(f"s_k{n}q{q}") for q in range(QUARTERS)] for n in range(2)]
            s_q1 = [sem(f"s_q1_{n}") for n in range(2)]
            s_q2 = [sem(f"s_q2_{n}") for n in range(2)]
            s_vh = [sem(f"s_vh{n}") for n in range(2)]
            st_ready = sem("st_ready")
            exp_done = sem("exp_done")
            pv_done = sem("pv_done")
            pool_added = sem("pool_added")
            ring_ready = sem("ring_ready")
            ring_free = [sem(f"ring_free{n}") for n in range(len(RING))]
            nm_zero = sem("nm_zero")
            nm_ready = sem("nm_ready")
            max_step = sem("max_step")
            sums_out = sem("sums_out")
            last_sums = sem("last_sums")
            s_xt = sem("s_xt")
            inverted = sem("inverted")
            divided = sem("divided")
            x_hi = sem("x_hi")
            x_lo = sem("x_lo")
            s_attst = [sem(f"s_attst{n}") for n in range(2)]

            def taken(eng, at):
                eng.wait_ge(ring_free[at[2]], at[1] + 1)

            OUT = 4
            xh = ks[0][:, 0:KT * T].rearrange("p (k n) -> p k n", n=T)
            xl = ks[0][:, KT * T:2 * KT * T].rearrange("p (k n) -> p k n", n=T)

            block = ctx.enter_context(nc.Block())

            def head_rows(ap, h):
                return ap[bass.ds(h * E, E), :]

            @block.sync
            def _(eng):
                def load_quarter(h, n, q):
                    cols = slice(q * QK, (q + 1) * QK)
                    for part, src in enumerate((kh_d, kh_d, kl_d)):
                        eng.dma_start(ks[n][part * E:(part + 1) * E, cols].bitcast(F32), head_rows(src, h)[:, cols])\
                           .then_inc(s_kq[n][q], 16)

                def load_q(h, tile, s):
                    for part, src in enumerate((qh_d, ql_d, qh_d)):
                        eng.dma_start(tile[part * E:(part + 1) * E, :].bitcast(F32), head_rows(src, h))\
                           .then_inc(s, 16)

                def load_v(h, n):
                    eng.dma_start(vh[n][:, :, :].rearrange("p t e -> p (t e)"), v_d[h, :, :]).then_inc(s_vh[n], 16)

                load_q(0, qmax[0], s_q1[0])
                load_quarter(0, 0, 0)
                load_quarter(0, 0, QUARTERS - 1)
                load_q(0, qexp[0], s_q2[0])
                load_q(1, qmax[1], s_q1[1])
                load_quarter(1, 1, 0)
                load_v(0, 0)
                for q in range(1, QUARTERS):
                    if q < QUARTERS - 1:
                        load_quarter(0, 0, q)
                    load_quarter(1, 1, q)

                def store(h, u):
                    taken(eng, ring_at(h + 1, SUM))
                    eng.dma_start(head_rows(att_d, h), att[u][0:E, :]).then_inc(s_attst[u], 16)
                    eng.dma_start(head_rows(den_d, h), att[u][E:2 * E, :]).then_inc(s_attst[u], 16)

                def load_outputs(xt, xd, heads, part):
                    for n in range(2):
                        eng.wait_ge(s_attst[n], 16 + 32 * len(range(n, heads, 2)))
                    eng.dma_start(xt, part(att_d)).then_inc(s_xt, 16)
                    eng.dma_start(xd, part(den_d)).then_inc(s_xt, 16)

                def step(i, u, first=False, has_next=True, has_next2=True):
                    h = i * 2 + u
                    if has_next2:
                        eng.wait_ge(nm_ready, h + 1)
                        load_q(h + 2, qmax[u], s_q1[u])
                    if has_next:
                        wait(eng, pv_done, PAIRS * h)
                        load_q(h + 1, qexp[1 - u], s_q2[1 - u])
                        load_v(h + 1, 1 - u)
                    if not has_next:
                        load_outputs(XN[:, 0:KT - 1, :], xd[:, 0:KT - 1, :], (KT - 1) * HT,
                                     lambda ap: rows(ap)[:, 0:KT - 1, :])
                    if not first:
                        store(h - 1, 1 - u)
                    if not has_next:
                        done = (HT - 1) * E
                        load_outputs(XN[0:done, KT - 1, :], xd[0:done, KT - 1, :], H - 1,
                                     lambda ap: ap[D - P:D - P + done, :])
                    if has_next2:
                        for q in range(QUARTERS):
                            eng.wait_ge(st_ready, PAIRS * h + PAIRS // QUARTERS * (q + 1))
                            load_quarter(h + 2, u, q)

                step(0, 0, first=True)
                step(0, 1)
                with eng.Fori(1, H // 2 - 1) as i:
                    step(i, 0)
                    step(i, 1)
                step(H // 2 - 1, 0, has_next2=False)
                step(H // 2 - 1, 1, has_next=False, has_next2=False)

            @block.gpsimd
            def _(eng):
                eng.memset(ones[:, :], 1.0).then_inc(const_c, 1)
                eng.memset(sel[:, :], 0.0).then_inc(const_c, 1)
                for j in range(4):
                    half = sel[:, j // 3 * E:(j // 3 + 1) * E]
                    eng.wait_ge(const_c, 2 + j)
                    eng.affine_select(out=half, in_=half, compare_op=ALU.not_equal, fill=1.0,
                                      base=-E * j, pattern=[[-1, E]], channel_multiplier=1).then_inc(const_c, 1)
                for n in range(2):
                    eng.wait_ge(const_c, 6 + n)
                    eng.memset(ks[n][3 * E:SROWS, :].bitcast(F32), 1.0).then_inc(const_c, 1)

                eng.wait_ge(const_c, 8)

                def step(h, u, use_over=True):
                    for k in range(1, POOL_PAIRS):
                        if k == 1 and use_over:
                            taken(eng, ring_at(h - 1, SUM))
                        eng.wait_ge(exp_done, h * PAIRS + (3 * k + 2) // 2 + 1)
                        tiles = [(3 * n + 1 + SLOTS * u) % (2 * SLOTS) for n in (0, k)]
                        pair = prob[:, tiles[1]:tiles[1] + 2, :]
                        if k == 1:
                            so_far = prob[:, tiles[0]:tiles[0] + 2, :]
                        else:
                            so_far = pool_sum[u][:, :, :]
                            eng.wait_ge(pool_added, h * POOL_ADDS + k - 1)
                        eng.tensor_tensor(pool_sum[u][:, :, :], so_far, pair, ALU.add).then_inc(pool_added, 1)

                step(0, 0, use_over=False)
                step(1, 1, use_over=False)
                with eng.Fori(1, H // 2) as i:
                    step(i * 2, 0)
                    step(i * 2 + 1, 1)

            @block.scalar
            def _(eng):
                def copy_out(h):
                    eng.wait_ge(pv_done, PAIRS * (h + 1))
                    eng.activation(osb[:, :], psum[:, OUT, :], ACT.Copy).then_inc(sums_out, 1)

                def step(h, u, first=False):
                    for p in range(PAIRS):
                        eng.wait_ge(st_ready, h * PAIRS + p + 1)
                        back, q = slot_before(u, p)
                        wait(eng, pv_done, h * PAIRS + p - back + 1)
                        if not (first and back > p):
                            eng.wait_ge(pool_added, (h * POOL_ADDS - (POOL_ADDS if back > p else 0)) + pool_adds(q))
                        at, b = 2 * slot_of(u, p), p % 2
                        eng.activation(prob[:, at:at + 2, :], psum[:, 2 * b:2 * b + 2, :], ACT.Exp)\
                           .then_inc(exp_done, 1)
                        if p == 1 and not first:
                            copy_out(h - 1)

                step(0, 0, first=True)
                step(1, 1)
                with eng.Fori(1, H // 2) as i:
                    step(i * 2, 0)
                    step(i * 2 + 1, 1)
                def high_output(k):
                    eng.wait_ge(divided, k + 1 if k < KT - 1 else KT + 1)
                    eng.activation(xh[:, k, :], XN[:, k, :], ACT.Copy).then_inc(x_hi, 1)

                for k in range(KT - 1):
                    high_output(k)
                copy_out(H - 1)
                high_output(KT - 1)

            @block.tensor
            def _(eng):
                def item(e, at, n, use=None, h=None):
                    _, _, kind, kc, qt = e
                    quarter, rest = divmod(kc, NCH // QUARTERS)
                    if kind == "max" and qt == 0 and rest == 0:
                        if quarter == 0:
                            eng.wait_ge(s_q1[n], 48 * use + 48)
                        eng.wait_ge(s_kq[n][quarter], 48 * use + 48)
                    if kind == "neg":
                        eng.wait_ge(nm_ready, h + 2)
                    if kind == "sum":
                        eng.wait_ge(sums_out, h)
                        eng.wait_ge(pool_added, h * POOL_ADDS)
                    bank = RING[at[2]]
                    wait(eng, ring_free[at[2]], at[1])
                    if kind == "neg":
                        for t in range(TT):
                            ins = eng.matmul(psum[3 * E:P, bank, t * P:(t + 1) * P], nm[:, t, :].bitcast(F32),
                                             ident[:, :], start=True, stop=True, tile_position=(0, 3 * E))
                    elif kind == "sum":
                        for j in range(2):
                            eng.matmul(psum[j * E:(j + 1) * E, bank, :], sel[:, j * E:(j + 1) * E], osb[:, :],
                                       start=True, stop=(j == 0), tile_position=(0, j * E))
                        for t in range(2):
                            ins = eng.matmul(psum[E:2 * E, bank, :], ones[:, :], pool_sum[n][:, t, :],
                                             start=False, stop=(t == 1), tile_position=(0, E))
                    else:
                        ins = eng.matmul(psum[:, bank, :], qmax[n][0:3 * E, qt * P:(qt + 1) * P],
                                         ks[n][0:3 * E, kc * CH:(kc + 1) * CH], start=True, stop=True)
                    ins.then_inc(ring_ready, 1)

                def summed(h, u, g, b):
                    p = 2 * g + b
                    eng.wait_ge(exp_done, h * PAIRS + p + 1)
                    for n in (2 * p, 2 * p + 1):
                        tile = prob[:, 2 * slot_of(u, p) + n % 2, :]
                        shares = [(n % 3, vh[u][:, n, :], n < 3, n >= KEYT - 3)]
                        if n % 3 == 0:
                            shares.append((3, ones[:, :], n == 0, n == KEYT - 1))
                        for j, left, start, stop in shares:
                            ins = eng.matmul(psum[j * E:(j + 1) * E, OUT, :], left, tile, start=start, stop=stop,
                                             tile_position=(0, j * E))
                    ins.then_inc(pv_done, 1)

                def step(i, u, first=False, last=False):
                    h = i * 2 + u
                    eng.wait_ge(s_q2[u], 48 * i + 48)
                    eng.wait_ge(s_vh[u], 16 * i + 16)
                    taken(eng, ring_at(-1 if first else h - 1, ITEMS - 1))
                    for e in schedule(first, last):
                        if e[0] == "st":
                            _, g, b = e
                            wait(eng, exp_done, h * PAIRS + 2 * g + b - 1)
                            for t in range(2):
                                key = (4 * g + 2 * b + t) * P
                                if first and key % QK == 0:
                                    eng.wait_ge(s_kq[0][key // QK], 48)
                                ins = eng.matmul(psum[:, 2 * b + t, :], ks[u][0:SROWS, key:key + P],
                                                 qexp[u][0:SROWS, :], start=True, stop=True)
                            ins.then_inc(st_ready, 1)
                        elif e[0] == "pv":
                            _, g, b = e
                            if g == NG - 1:
                                summed(h - 1, 1 - u, g, b)
                            else:
                                if g == 0 and b == 0:
                                    wait(eng, sums_out, h)
                                summed(h, u, g, b)
                        else:
                            item(e, ring_at(h, e[1]), 1 - u, i + u, h)

                for k, it in LATE:
                    if it[1:] == (NCH - 2, 0):
                        eng.wait_ge(s_kq[0][QUARTERS - 1], 48)
                    item(("item", number(k)) + it, ring_at(-1, number(k)), 0, 0, -1)
                item(("item", ITEMS - 1, "neg", 0, 0), ring_at(-1, ITEMS - 1), 0, h=-1)
                eng.wait_ge(const_c, 8)
                step(0, 0, first=True)
                step(0, 1)
                with eng.Fori(1, H // 2 - 1) as i:
                    step(i, 0)
                    step(i, 1)
                step(H // 2 - 1, 0)
                step(H // 2 - 1, 1, last=True)
                summed(H - 1, 1, NG - 1, 0)
                summed(H - 1, 1, NG - 1, 1)

                def project(t, width_tiles):
                    for k in width_tiles:
                        eng.wait_ge(x_hi, k + 1)
                        eng.wait_ge(x_lo, k + 1)
                        for n, (left, right) in enumerate(((xh, AH), (xh, AL), (xl, AH))):
                            ins = eng.matmul(psum[:, t, :], left[:, k, t * P:(t + 1) * P], right[:, k, :],
                                             start=(k == 0 and n == 0), stop=(k == KT - 1 and n == 2))
                    return ins

                early = range(KT - 1)
                for t in range(TT // 2):
                    project(t, early)
                eng.wait_ge(sums_out, H)
                eng.wait_ge(pool_added, H * POOL_ADDS)
                taken(eng, ring_at(H - 1, SUM))
                rows_of_last = slice(P - E, P)
                for j, bank in enumerate((OUT, RING[0])):
                    eng.matmul(psum[rows_of_last, bank, :], sel[:, j * E:(j + 1) * E], osb[:, :],
                               start=True, stop=(j == 0), tile_position=(0, P - E))
                for t in range(2):
                    ins = eng.matmul(psum[rows_of_last, RING[0], :], ones[:, :], pool_sum[1][:, t, :],
                                     start=False, stop=(t == 1), tile_position=(0, P - E))
                ins.then_inc(last_sums, 1)
                for t in range(TT // 2, TT):
                    project(t, early)
                for t in range(TT):
                    project(t, [KT - 1]).then_inc(pe_out, 1)

            @block.vector
            def _(eng):
                eng.memset(nm[:, :, :].bitcast(F32), 0.0).then_inc(nm_zero, 1)
                for n in range(2):
                    eng.memset(att[n][:, :], 0.0).then_inc(s_attst[n], 16)

                def take(e, at, n, stores=None):
                    _, _, kind, kc, qt = e
                    src = psum[:, RING[at[2]], :]
                    eng.wait_ge(ring_ready, at[0] + 1)
                    if kind == "max":
                        ins = eng.tensor_reduce(mx[:, qt, kc:kc + 1], src, AX.X, ALU.max)
                    elif kind == "neg":
                        ins = eng.tensor_copy(qexp[n][3 * E:SROWS, :], psum[3 * E:SROWS, RING[at[2]], :])
                    else:
                        eng.wait_ge(s_attst[n], 32 * stores + 16)
                        ins = eng.tensor_copy(att[n][:, :], src[0:2 * E, :])
                    ins.then_inc(ring_free[at[2]], 1)

                def negate_max(h):
                    for k in range(len(RING)):
                        taken(eng, ring_at(h - 1, ITEMS - 2 - k))
                    eng.tensor_reduce(m4[:, :], mx[:, :, :], AX.X, ALU.max).then_inc(max_step, 1)
                    eng.wait_ge(max_step, 2 * h + 1)
                    eng.tensor_scalar(nm[:, :, 0], m4[:, :], -1.0, None, ALU.mult).then_inc(max_step, 1)
                    eng.wait_ge(max_step, 2 * h + 2)
                    eng.scalar_tensor_tensor(out=nm[:, :, 1], in0=m4[:, :], scalar=-1.0,
                                             in1=nm[:, :, 0].bitcast(F32), op0=ALU.mult, op1=ALU.subtract)\
                       .then_inc(nm_ready, 1)

                def step(i, u, first=False, last=False):
                    h = i * 2 + u
                    for e in schedule(first, last):
                        if e[0] == "item":
                            if e[2] == "neg":
                                negate_max(h + 1)
                            take(e, ring_at(h, e[1]), 1 - u, i + u - 1)

                eng.wait_ge(nm_zero, 1)
                for k, it in LATE:
                    take(("item", number(k)) + it, ring_at(-1, number(k)), 0)
                negate_max(0)
                take(("item", ITEMS - 1, "neg", 0, 0), ring_at(-1, ITEMS - 1), 0)
                step(0, 0, first=True)
                step(0, 1)
                with eng.Fori(1, H // 2 - 1) as i:
                    step(i, 0)
                    step(i, 1)
                step(H // 2 - 1, 0)
                step(H // 2 - 1, 1, last=True)

                def divide(xt, outputs, xd, denominators, n):
                    eng.reciprocal(xd, denominators).then_inc(inverted, 1)
                    eng.wait_ge(inverted, n)
                    eng.tensor_tensor(xt, outputs, xd, ALU.mult).then_inc(divided, 1)

                def low_output(k):
                    eng.wait_ge(x_hi, k + 1)
                    eng.tensor_tensor(xl[:, k, :], XN[:, k, :], xh[:, k, :].bitcast(F32), ALU.subtract)\
                       .then_inc(x_lo, 1)

                eng.wait_ge(s_xt, 32)
                for k in range(KT - 1):
                    divide(XN[:, k, :], XN[:, k, :], xd[:, k, :], xd[:, k, :], k + 1)
                eng.wait_ge(s_xt, 64)
                outs, dens = XN[0:P - E, KT - 1, :], xd[0:P - E, KT - 1, :]
                divide(outs, outs, dens, dens, KT)
                for t in range(TT):
                    ins = eng.tensor_tensor(X[:, t, :], X[:, t, :], brow[:, 1, :], ALU.add)
                link(eng, ins)
                for k in range(KT - 1):
                    low_output(k)
                eng.wait_ge(last_sums, 1)
                divide(XN[P - E:P, KT - 1, :], psum[P - E:P, OUT, :], xd[P - E:P, KT - 1, :],
                       psum[P - E:P, RING[0], :], KT + 1)
                low_output(KT - 1)

        with ExitStack() as ctx:
            sb3 = alloc(ctx)
            raw = [sb3(f"raw{n}", [P, KT, D]) for n in range(2)]
            bh = [sb3(f"bh{n}", [P, KT, D], F32R) for n in range(4)]
            bl = [sb3(f"bl{n}", [P, KT, D], F32R) for n in range(4)]
            gate = sb3("gate", [P, KT, T])
            y = sb3("y", [P, KT, T])
            hf = sb3("hf", [P, KT, T])
            hh = [sb3(f"hh{n}", [P, KT, T], F32R) for n in range(2)]
            hl = [sb3(f"hl{n}", [P, KT, T], F32R) for n in range(2)]
            graw = sb3("graw", [P, KT, NEXP])
            gh = sb3("gh", [P, KT, NEXP], F32R)
            gl = sb3("gl", [P, KT, NEXP], F32R)
            ss = sb3("ss", [P, TT])
            lr = sb3("lr", [P, TT])
            pr = sb3("pr", [P, TT, NEXP])
            pe = sb3("pe", [P, TT, NEXP])
            r1 = sb3("r1", [P, TT])
            cmp_ = sb3("cmp", [P, TT, NEXP, NEXP])
            eq_ = sb3("eq", [P, TT, NEXP, NEXP])
            before = sb3("before", [P, NEXP, NEXP])
            rank = sb3("rank", [P, TT, NEXP])
            wt = sb3("wt", [P, TT, NEXP])

            s_gw = sem("s_gw")
            s_raw = [sem(f"s_raw{n}") for n in range(2)]
            act_bh = sem("act_bh")
            pool_bl = sem("pool_bl")
            act_gh = sem("act_gh")
            dve_gl = sem("dve_gl")
            act_sig = sem("act_sig")
            dve_y = sem("dve_y")
            dve_qy = sem("dve_qy")
            dve_logits = sem("dve_logits")
            act_pe = sem("act_pe")
            act_sg = sem("act_sg")
            dve_gu = sem("dve_gu")
            act_hs = sem("act_hs")
            dve_hs = sem("dve_hs")
            dve_x3 = sem("dve_x3")
            before_set = sem("before_set")
            pe_h = sem("pe_h")
            pe_y = sem("pe_y")
            act_silu = sem("act_silu")
            act_hh = sem("act_hh")
            dve_hl = sem("dve_hl")
            dve_acc = sem("dve_acc")
            s_out = sem("s_out")

            NS = 6
            WA, WKV, WQ, SG, SU, SD = range(NS)

            def slot(n):
                return n % 4

            W1 = (slot(NS), slot(NS + 1))
            W2 = (slot(NS + 2), slot(NS + 3))

            OUT_WE, OUT_A, OUT_KV, OUT_Q = TT, 2 * TT, 3 * TT, 4 * TT
            OUT_LOG, OUT_G, OUT_U, OUT_D = 4 * TT + 1, 5 * TT + 1, 6 * TT + 1, 7 * TT + 1
            last_use = (OUT_A, OUT_KV, OUT_Q, OUT_G, OUT_U, OUT_D)

            block = ctx.enter_context(nc.Block())

            def split_load(eng, n, src, r):
                wait(eng, pool_bl, n - 1)
                eng.dma_start(raw[r][:, :, :], src).then_inc(s_raw[r], 16)

            def split_hi(eng, r, sl, use, used_by, count):
                eng.wait_ge(s_raw[r], 16 * use + 16)
                wait(eng, used_by, count)
                eng.activation(bh[sl][:, :, :], raw[r][:, :, :], ACT.Copy).then_inc(act_bh, 1)

            def split_lo(eng, n, r, sl):
                eng.wait_ge(act_bh, n + 1)
                eng.tensor_tensor(bl[sl][:, :, :], raw[r][:, :, :], bh[sl][:, :, :].bitcast(F32), ALU.subtract)\
                   .then_inc(pool_bl, 1)

            @block.sync
            def _(eng):
                straight = [rows(w_qkvaT)[:, :, 2 * D:3 * D], rows(w_qkvaT)[:, :, D:2 * D],
                            rows(w_qkvaT)[:, :, 0:D], rows(sguT)[:, :, 0:D], rows(sguT)[:, :, D:2 * D],
                            rows(sdownT), rows(w1T[0, :, :]), rows(w1T[1, :, :]), rows(w2T[0, :, :])]
                for n, src in enumerate(straight):
                    split_load(eng, n, src, n % 2)
                    if n == 1:
                        eng.dma_start(graw[:, :, :], rows(gate_wT)).then_inc(s_gw, 16)
                with eng.Fori(0, NEXP - 2) as e:
                    split_load(eng, e * 2 + NS + 3, rows(w1T[e + 2, :, :]), (NS + 3) % 2)
                    split_load(eng, e * 2 + NS + 4, rows(w2T[e + 1, :, :]), NS % 2)
                split_load(eng, 2 * (NEXP - 2) + NS + 3, rows(w2T[NEXP - 1, :, :]), (NS + 3) % 2)
                for t in range(TT):
                    eng.wait_ge(dve_acc, TT * (NEXP - 1) + t + 1)
                    eng.dma_start(out[t * P:(t + 1) * P, :], X[:, t, :]).then_inc(s_out, 16)
                eng.wait_ge(s_out, 16 * TT)

            @block.gpsimd
            def _(eng):
                eng.memset(before[:, :, :], 0.0).then_inc(before_set, 1)
                eng.wait_ge(before_set, 1)
                eng.affine_select(out=before[:, :, :], in_=before[:, :, :], compare_op=ALU.is_ge, fill=1.0, base=0,
                                  pattern=[[-1, NEXP], [1, NEXP]], channel_multiplier=0).then_inc(before_set, 1)
                for n in range(NS + 3):
                    split_lo(eng, n, n % 2, slot(n))
                with eng.Fori(0, NEXP // 2 - 1) as i:
                    for u in range(2):
                        n = (i * 2 + u) * 2 + NS + 3
                        split_lo(eng, n, (NS + 3) % 2, W1[u])
                        split_lo(eng, n + 1, NS % 2, W2[1 - u])
                split_lo(eng, 2 * (NEXP - 2) + NS + 3, (NS + 3) % 2, W2[1])

            @block.scalar
            def _(eng):
                def hi(n):
                    split_hi(eng, n % 2, slot(n), n // 2, pe_out, last_use[n - 4] if n >= 4 else 0)

                root_act(eng, 2)
                root_act(eng, 3)
                hi(0)
                hi(1)
                for k in range(KT):
                    eng.wait_ge(pe_tr, KT + k + 1)
                    eng.activation(AH[:, k, :], psum[:, k, :], ACT.Copy, scale=bcol[:, 2, k:k + 1]).then_inc(act_hi, 1)
                hi(2)
                eng.wait_ge(s_gw, 16)
                eng.activation(gh[:, :, :], graw[:, :, :], ACT.Copy).then_inc(act_gh, 1)
                preload(eng, ACT.Sigmoid)
                for m in range(KT):
                    eng.wait_ge(pe_out, OUT_WE + m + 1)
                    eng.activation(gate[:, m, :], psum[:, m, :], ACT.Sigmoid).then_inc(act_sig, 1)
                for n in (3, 4, 5, 6):
                    hi(n)
                root_act(eng, 4)
                for k in range(KT):
                    eng.wait_ge(pe_tr, 3 * KT + k + 1)
                    eng.activation(AH[:, k, :], psum[:, k, :], ACT.Copy).then_inc(act_hi, 1)
                preload(eng, ACT.Exp)
                eng.wait_ge(dve_logits, 1)
                eng.activation(pe[:, :, :], pr[:, :, :], ACT.Exp).then_inc(act_pe, 1)
                preload(eng, ACT.Silu)
                for m in range(KT):
                    eng.wait_ge(pe_out, OUT_LOG + m + 1)
                    eng.activation(gate[:, m, :], psum[:, m, :], ACT.Silu).then_inc(act_sg, 1)
                for m in range(KT):
                    eng.wait_ge(dve_gu, m + 1)
                    eng.activation(hh[1][:, m, :], y[:, m, :], ACT.Copy).then_inc(act_hs, 1)
                hi(NS + 1)
                hi(NS + 2)

                def silu(e, u):
                    wait(eng, dve_hl, KT * e)
                    wait(eng, pe_y, TT * (e - 1))
                    if isinstance(e, int) and e == 1:
                        eng.wait_ge(pe_out, OUT_D)
                    for m in range(KT):
                        eng.wait_ge(pe_h, KT * e + m + 1)
                        eng.activation(hf[:, m, :], psum[:, m, :], ACT.Silu).then_inc(act_silu, 1)
                    for m in range(KT):
                        eng.wait_ge(act_silu, KT * e + m + 1)
                        eng.activation(hh[u][:, m, :], hf[:, m, :], ACT.Copy).then_inc(act_hh, 1)

                silu(0, 0)

                def expert(e, u, w1=True):
                    if w1:
                        split_hi(eng, (NS + 3) % 2, W1[u], e + (NS + 3) // 2, pe_h, KT * (e + 1))
                    r, use = (NS % 2, e + (NS + 4) // 2) if w1 else ((NS + 3) % 2, e + (NS + 3) // 2)
                    if isinstance(e, int) and e == 0:
                        split_hi(eng, r, W2[1 - u], use, pe_out, OUT_D)
                    else:
                        split_hi(eng, r, W2[1 - u], use, pe_y, TT * e)
                    silu(e + 1, 1 - u)

                expert(0, 0)
                expert(1, 1)
                with eng.Fori(1, NEXP // 2 - 1) as i:
                    expert(i * 2, 0)
                    expert(i * 2 + 1, 1)
                expert(NEXP - 2, 0, w1=False)

            @block.tensor
            def _(eng):
                def weights(n):
                    eng.wait_ge(pool_bl, n + 1)
                    return bh[slot(n)], bl[slot(n)]

                transpose_pe(eng, TT)
                for b, n in ((0, WA), (KT, WKV), (0, WQ)):
                    h_, l_ = weights(n)
                    for m in range(KT):
                        if n == WQ:
                            eng.wait_ge(act_sig, m + 1)
                        product3(eng, psum[:, b + m, :], h_, l_, AH, AL, slice(m * P, (m + 1) * P),
                                 ready=(act_hi, dve_lo, KT) if n == WA else None)\
                            .then_inc(pe_out, 1)
                for k in range(KT):
                    eng.wait_ge(dve_qy, k + 1)
                    for t in range(TT):
                        ins = eng.transpose(psum[:, 4 + t, k * P:(k + 1) * P], y[:, k, t * P:(t + 1) * P], ident[:, :])
                        if k == KT - 1:
                            ins.then_inc(pe_tr, 1)
                transpose_pe(eng, 2 * TT)
                eng.wait_ge(act_gh, 1)
                eng.wait_ge(dve_gl, 1)
                for t in range(TT):
                    ins = product3(eng, psum[:, 4, t * NEXP:(t + 1) * NEXP], AH, AL, gh, gl, slice(t * P, (t + 1) * P),
                                   ready=(act_hi, dve_lo, 2 * KT))
                ins.then_inc(pe_out, 1)
                for b, n in ((0, SG), (KT, SU)):
                    h_, l_ = weights(n)
                    if n == SU:
                        eng.wait_ge(dve_logits, 1)
                    for m in range(KT):
                        product3(eng, psum[:, b + m, :], h_, l_, AH, AL, slice(m * P, (m + 1) * P))\
                            .then_inc(pe_out, 1)
                def first(e, u):
                    if isinstance(e, int) and e == 0:
                        eng.wait_ge(pool_bl, NS + 1)
                        eng.wait_ge(act_sg, KT)
                    else:
                        eng.wait_ge(pool_bl, e * 2 + NS)
                    for m in range(KT):
                        wait(eng, act_silu, KT * (e - 1) + m + 1)
                        ins = product3(eng, psum[:, m, :], bh[W1[u]], bl[W1[u]], AH, AL, slice(m * P, (m + 1) * P))
                        ins.then_inc(pe_h, 1)

                def second(e, u, last=False):
                    eng.wait_ge(pool_bl, e * 2 + NS + 3 - (1 if last else 0))
                    eng.wait_ge(dve_hl, KT * (e + 1))
                    eng.wait_ge(act_hh, KT * (e + 1))
                    for t in range(TT):
                        if isinstance(e, int) and e == 0:
                            eng.wait_ge(dve_x3, t + 1)
                        wait(eng, dve_acc, TT * (e - 1) + t + 1)
                        ins = product3(eng, psum[:, 4 + t, :], hh[u], hl[u], bh[W2[u]], bl[W2[u]],
                                       slice(t * P, (t + 1) * P))
                        ins.then_inc(pe_y, 1)

                first(0, 0)
                h_, l_ = weights(SD)
                eng.wait_ge(dve_gu, KT)
                for t in range(TT):
                    product3(eng, psum[:, 4 + t, :], hh[1], hl[1], h_, l_, slice(t * P, (t + 1) * P),
                             ready=(act_hs, dve_hs, 0)).then_inc(pe_out, 1)

                def expert(e, u, last=False):
                    if not last:
                        first(e + 1, 1 - u)
                    second(e, u, last)

                expert(0, 0)
                expert(1, 1)
                with eng.Fori(1, NEXP // 2 - 1) as i:
                    expert(i * 2, 0)
                    expert(i * 2 + 1, 1)
                expert(NEXP - 2, 0)
                expert(NEXP - 1, 1, last=True)

            @block.vector
            def _(eng):

                def add_projection(t):
                    eng.wait_ge(pe_out, t + 1)
                    return eng.tensor_tensor(X[:, t, :], X[:, t, :], psum[:, t, :], ALU.add)

                row_moments_dve(eng, add_projection)
                eng.tensor_scalar(ve[:, :], mv[:, :, 1], LN_EPS, None, ALU.add).then_inc(dve_ve, 1)
                inverse_root_dve(eng)
                link(eng, eng.tensor_copy(lr[:, :], rs[:, :]))
                link(eng, eng.tensor_tensor(ss[:, :], lr[:, :], lr[:, :], ALU.mult))
                link(eng, eng.tensor_tensor(ss[:, :], ss[:, :], mv[:, :, 1], ALU.mult))
                eng.tensor_scalar(ve[:, :], ss[:, :], NORM_EPS * NORM_EPS / D, None, ALU.max).then_inc(dve_ve, 1)
                inverse_root_dve(eng)
                link(eng, eng.tensor_tensor(lr[:, :], lr[:, :], rs[:, :], ALU.mult))
                for t in range(TT):
                    eng.tensor_scalar(XN[:, t, :], X[:, t, :], mv[:, t, 0:1], lr[:, t:t + 1],
                                      ALU.subtract, ALU.mult).then_inc(dve_xn, 1)
                for k in range(KT):
                    eng.wait_ge(act_hi, KT + k + 1)
                    eng.scalar_tensor_tensor(out=AL[:, k, :], in0=psum[:, k, :], scalar=bcol[:, 2, k:k + 1],
                                             in1=AH[:, k, :].bitcast(F32), op0=ALU.mult, op1=ALU.subtract)\
                       .then_inc(dve_lo, 1)
                eng.wait_ge(act_gh, 1)
                eng.tensor_tensor(gl[:, :, :], graw[:, :, :], gh[:, :, :].bitcast(F32), ALU.subtract)\
                   .then_inc(dve_gl, 1)
                for m in range(KT):
                    eng.wait_ge(act_sig, m + 1)
                    eng.wait_ge(pe_out, OUT_A + m + 1)
                    eng.tensor_tensor_scan(y[:, m, :], gate[:, m, :], psum[:, KT + m, :], 0.0, ALU.mult, ALU.add)\
                       .then_inc(dve_y, 1)
                for m in range(KT):
                    eng.wait_ge(dve_y, m + 1)
                    eng.wait_ge(pe_out, OUT_KV + m + 1)
                    eng.tensor_tensor(y[:, m, :], y[:, m, :], psum[:, m, :], ALU.mult).then_inc(dve_qy, 1)

                def add_recurrence(t):
                    eng.wait_ge(pe_tr, 2 * KT + t + 1)
                    return eng.tensor_tensor(X[:, t, :], X[:, t, :], psum[:, 4 + t, :], ALU.add)

                layer_norm_dve(eng, add_recurrence)
                for k in range(KT):
                    eng.wait_ge(act_hi, 2 * KT + k + 1)
                    eng.tensor_tensor(AL[:, k, :], psum[:, k, :], AH[:, k, :].bitcast(F32), ALU.subtract)\
                       .then_inc(dve_lo, 1)

                def over_experts(ap):
                    return ap.unsqueeze(2).to_broadcast([P, TT, NEXP])

                logits = psum[:, 4, 0:TT * NEXP].rearrange("p (t e) -> p t e", e=NEXP)
                eng.wait_ge(pe_out, OUT_LOG)
                link(eng, eng.tensor_reduce(r1[:, :], logits, AX.X, ALU.max))
                eng.tensor_tensor(pr[:, :, :], logits, over_experts(r1[:, :]), ALU.subtract).then_inc(dve_logits, 1)
                for m in range(KT):
                    eng.wait_ge(act_sg, m + 1)
                    eng.wait_ge(pe_out, OUT_G + m + 1)
                    eng.tensor_tensor(y[:, m, :], gate[:, m, :], psum[:, KT + m, :], ALU.mult).then_inc(dve_gu, 1)
                for m in range(KT):
                    eng.wait_ge(act_hs, m + 1)
                    eng.tensor_tensor(hl[1][:, m, :], y[:, m, :], hh[1][:, m, :].bitcast(F32), ALU.subtract)\
                       .then_inc(dve_hs, 1)
                eng.wait_ge(act_pe, 1)
                link(eng, eng.tensor_reduce(r1[:, :], pe[:, :, :], AX.X, ALU.add))
                link(eng, eng.reciprocal(t0[:, :], r1[:, :]))
                link(eng, eng.tensor_tensor(pr[:, :, :], pe[:, :, :], over_experts(t0[:, :]), ALU.mult))
                mine = pr[:, :, :].unsqueeze(3).to_broadcast([P, TT, NEXP, NEXP])
                other = pr[:, :, :].unsqueeze(2).to_broadcast([P, TT, NEXP, NEXP])
                link(eng, eng.tensor_tensor(cmp_[:, :, :, :], other, mine, ALU.is_gt))
                link(eng, eng.tensor_tensor(eq_[:, :, :, :], other, mine, ALU.is_equal))
                eng.wait_ge(before_set, 2)
                link(eng, eng.tensor_tensor(eq_[:, :, :, :], eq_[:, :, :, :],
                                            before[:, :, :].unsqueeze(1).to_broadcast([P, TT, NEXP, NEXP]), ALU.mult))
                link(eng, eng.tensor_tensor(cmp_[:, :, :, :], cmp_[:, :, :, :], eq_[:, :, :, :], ALU.add))
                link(eng, eng.tensor_reduce(rank[:, :, :], cmp_[:, :, :, :], AX.X, ALU.add))
                link(eng, eng.tensor_scalar(rank[:, :, :], rank[:, :, :], float(TOPK), None, ALU.is_lt))
                link(eng, eng.tensor_tensor(wt[:, :, :], pr[:, :, :], rank[:, :, :], ALU.mult))
                link(eng, eng.tensor_reduce(r1[:, :], wt[:, :, :], AX.X, ALU.add))
                link(eng, eng.reciprocal(t0[:, :], r1[:, :]))
                link(eng, eng.tensor_tensor(wt[:, :, :], wt[:, :, :], over_experts(t0[:, :]), ALU.mult))
                for t in range(TT):
                    eng.wait_ge(pe_out, OUT_U + t + 1)
                    eng.tensor_tensor(X[:, t, :], X[:, t, :], psum[:, 4 + t, :], ALU.add).then_inc(dve_x3, 1)

                def split(e, u):
                    for m in range(KT):
                        eng.wait_ge(act_hh, KT * e + m + 1)
                        eng.tensor_tensor(hl[u][:, m, :], hf[:, m, :], hh[u][:, m, :].bitcast(F32), ALU.subtract)\
                           .then_inc(dve_hl, 1)

                def expert(e, u, last=False):
                    if not last:
                        split(e + 1, 1 - u)
                    for t in range(TT):
                        eng.wait_ge(pe_y, TT * e + t + 1)
                        if isinstance(e, int) and e == 0:
                            eng.wait_ge(dve_x3, t + 1)
                        else:
                            eng.wait_ge(dve_acc, TT * (e - 1) + t + 1)
                        eng.scalar_tensor_tensor(out=X[:, t, :], in0=psum[:, 4 + t, :],
                                                 scalar=wt[:, t, :][:, bass.ds(e, 1)], in1=X[:, t, :],
                                                 op0=ALU.mult, op1=ALU.add).then_inc(dve_acc, 1)

                split(0, 0)
                expert(0, 0)
                expert(1, 1)
                with eng.Fori(1, NEXP // 2 - 1) as i:
                    expert(i * 2, 0)
                    expert(i * 2 + 1, 1)
                expert(NEXP - 2, 0)
                expert(NEXP - 1, 1, last=True)


def kernel(**inputs):
    import numpy as np
    import concourse.bacc as bacc
    from concourse.bass_utils import run_bass_kernel_spmd

    def columns(v):
        return np.ascontiguousarray(np.asarray(v).reshape(KT, P).T)

    def transposed(a):
        return np.ascontiguousarray(np.swapaxes(np.asarray(a), -1, -2))

    laid_out = {
        "x": np.asarray(inputs["x"])[0],
        "ctxT": transposed(inputs["ctx_1024"])[0],
        "wq": inputs["L0_xattn_Wq"], "bq": columns(inputs["L0_xattn_bq"]),
        "wk": inputs["L0_xattn_Wk"], "bk": columns(inputs["L0_xattn_bk"]),
        "wv": inputs["L0_xattn_Wv"], "bv": np.asarray(inputs["L0_xattn_bv"]).reshape(1, D),
        "we": inputs["L0_xattn_We"], "be": np.asarray(inputs["L0_xattn_be"]).reshape(1, D),
        "w_qkvaT": transposed(inputs["L0_attn_W_qkva"]), "gamma": columns(inputs["L0_attn_gamma"]),
        "gate_wT": transposed(inputs["L0_ffn_gate_w"]),
        "w1T": transposed(inputs["L0_ffn_w1"]), "w2T": transposed(inputs["L0_ffn_w2"]),
        "sguT": transposed(inputs["L0_ffn_shared_gu"]), "sdownT": transposed(inputs["L0_ffn_shared_down"]),
    }
    nc = bacc.Bacc("TRN2", target_bir_lowering=False, num_devices=1)
    arrays, args = {}, []
    for name, a in laid_out.items():
        a = np.ascontiguousarray(a)
        arrays[name + "_dram"] = a
        args.append(nc.dram_tensor(name + "_dram", a.shape, mybir.dt.from_np(a.dtype), kind="ExternalInput").ap())
    args.append(nc.dram_tensor("out_dram", (T, D), F32, kind="ExternalOutput").ap())
    perceiver_program(nc, *args)
    r = run_bass_kernel_spmd(nc, [arrays], core_ids=[0])
    return np.asarray(r.results[0]["out_dram"]).reshape(1, T, D)
```
